# Optimizing a Trainium2 kernel written in Bass

```python
import numpy as np
import jax
import jax.numpy as jnp

def _softmax(x, axis=-1):
    return jax.nn.softmax(x, axis=axis)

def _gelu(x):
    return jax.nn.gelu(x, approximate=True)

def _silu(x):
    return jax.nn.silu(x)

def _sigmoid(x):
    return jax.nn.sigmoid(x)

def _layernorm(x, axis=-1, eps=1e-05):
    m = jnp.mean(x, axis=axis, keepdims=True)
    v = jnp.var(x, axis=axis, keepdims=True)
    return (x - m) / jnp.sqrt(v + eps)

def _scatter_add(tgt, idx, src, axis=0):
    return tgt.at[idx].add(src)

def _segment_sum(src, seg, n):
    return jax.ops.segment_sum(src, seg, n)
kernel_name = 'mk_metaformer_d1_conv_nchw256_r2_aac45d'

def setup_inputs(seed: int=0):
    np.random.seed(seed)
    _w = jnp.asarray

    def _rec_inputs():
        import jax
        import jax.numpy as jnp
        _gk = jax.random.key(seed)
        x = -0.000125 + 0.9999 * jax.random.normal(jax.random.fold_in(_gk, 1), (2, 128, 128, 128), jnp.float32)
        return x
    x = _rec_inputs()

    def _L0_conv_setup():
        import jax, jax.numpy as jnp
        import numpy as np
        B, C, H, W = (2, 128, 128, 128)
        NH = 8
        DK = C // NH
        WS = 8
        SS = 4
        L = WS * WS
        NW = H // WS * (W // WS)

        def _relative_position_index(ws):
            coords = np.stack(np.meshgrid(np.arange(ws), np.arange(ws), indexing='ij'))
            cf = coords.reshape(2, -1)
            rel = cf[:, :, None] - cf[:, None, :]
            rel = rel.transpose(1, 2, 0).astype(np.int64)
            rel[..., 0] += ws - 1
            rel[..., 1] += ws - 1
            rel[..., 0] *= 2 * ws - 1
            return rel.sum(-1)

        def _shift_attn_mask(h, w, ws, ss):
            img = np.zeros((h, w), dtype=np.float32)
            slices = (slice(0, -ws), slice(-ws, -ss), slice(-ss, None))
            cnt = 0
            for hs in slices:
                for wsl in slices:
                    img[hs, wsl] = cnt
                    cnt += 1
            m = img.reshape(h // ws, ws, w // ws, ws).transpose(0, 2, 1, 3).reshape(-1, ws * ws)
            diff = m[:, None, :] - m[:, :, None]
            return np.where(diff != 0, -100.0, 0.0).astype(np.float32)
        _REL_IDX = jnp.asarray(_relative_position_index(WS).reshape(-1))
        _ATTN_MASK = jnp.asarray(_shift_attn_mask(H, W, WS, SS))

        def _partition(t):
            t = t.reshape(B, C, H // WS, WS, W // WS, WS)
            t = t.transpose(0, 2, 4, 1, 3, 5)
            return t.reshape(B * NW, NH, DK, L)
        key = jax.random.key(seed)
        ks = jax.random.split(key, 5)
        return {'x': jax.random.normal(ks[0], (B, C, H, W), dtype=jnp.float32), 'Wq': jax.random.normal(ks[1], (C, C), dtype=jnp.float32) * 0.02, 'bq': jnp.zeros((C,), dtype=jnp.float32), 'Wkv': jax.random.normal(ks[2], (2 * C, C), dtype=jnp.float32) * 0.02, 'bkv': jnp.zeros((2 * C,), dtype=jnp.float32), 'Wproj': jax.random.normal(ks[3], (C, C), dtype=jnp.float32) * 0.02, 'bproj': jnp.zeros((C,), dtype=jnp.float32), 'bias_table': jax.random.normal(ks[4], ((2 * WS - 1) ** 2, NH), dtype=jnp.float32) * 0.02}
    _L0_conv_all = _L0_conv_setup()
    _L0_conv_in = {k: v for k, v in _L0_conv_all.items() if k in ('Wq', 'bq', 'Wkv', 'bkv', 'Wproj', 'bproj', 'bias_table')}
    del _L0_conv_all

    def _L0_ffn_setup():
        import jax, jax.numpy as jnp
        import numpy as np
        B, N, D = (16, 2048, 128)
        NUM_EXPERTS, TOP_K, HEADS = (4, 2, 4)
        N_EDGES = 524288
        LN_EPS = 1e-05

        def _layernorm(x, g, b):
            mu = x.mean(-1, keepdims=True)
            var = ((x - mu) ** 2).mean(-1, keepdims=True)
            return (x - mu) * jax.lax.rsqrt(var + LN_EPS) * g + b

        def _forward(x, edge_index, W_gat, att_src, att_dst, b_gat, ln_gamma, ln_beta, W1, b1, W2, b2):
            Bc, Nc, Dc = x.shape
            M = Bc * Nc
            x_flat = x.reshape(M, Dc)
            h = (x_flat @ W_gat).reshape(M, HEADS, NUM_EXPERTS)
            loops = jnp.arange(M, dtype=edge_index.dtype)
            src = jnp.concatenate([edge_index[0], loops])
            dst = jnp.concatenate([edge_index[1], loops])
            a_src = (h * att_src).sum(-1)
            a_dst = (h * att_dst).sum(-1)
            e = jax.nn.leaky_relu(a_src[src] + a_dst[dst], negative_slope=0.2)
            e_max = jax.ops.segment_max(e, dst, num_segments=M)
            ee = jnp.exp(e - e_max[dst])
            denom = jax.ops.segment_sum(ee, dst, num_segments=M)
            alpha = ee / (denom[dst] + 1e-16)
            msg = h[src] * alpha[:, :, None]
            agg = jax.ops.segment_sum(msg, dst, num_segments=M).reshape(M, HEADS * NUM_EXPERTS) + b_gat
            scores = _layernorm(agg, ln_gamma, ln_beta).reshape(M, HEADS, NUM_EXPERTS).mean(1)
            scores = scores.reshape(Bc, Nc, NUM_EXPERTS)
            topk_s, topk_i = jax.lax.top_k(scores, TOP_K)
            w = jax.nn.softmax(topk_s, axis=-1)
            out = jnp.zeros_like(x)
            for ei in range(NUM_EXPERTS):
                g = jnp.where(topk_i == ei, w, 0.0).sum(-1)
                hh = jax.nn.gelu(x @ W1[ei] + b1[ei], approximate=False)
                out = out + g[..., None] * (hh @ W2[ei] + b2[ei])
            return out
        key = jax.random.key(seed)
        ks = jax.random.split(key, 8)
        s = 0.05
        return {'x': jax.random.normal(ks[0], (B, N, D), jnp.float32), 'W_gat': jax.random.normal(ks[1], (D, HEADS * NUM_EXPERTS), jnp.float32) * s, 'att_src': jax.random.normal(ks[2], (HEADS, NUM_EXPERTS), jnp.float32) * s, 'att_dst': jax.random.normal(ks[3], (HEADS, NUM_EXPERTS), jnp.float32) * s, 'b_gat': jnp.zeros((HEADS * NUM_EXPERTS,), jnp.float32), 'ln_gamma': jnp.ones((HEADS * NUM_EXPERTS,), jnp.float32), 'ln_beta': jnp.zeros((HEADS * NUM_EXPERTS,), jnp.float32), 'W1': jax.random.normal(ks[4], (NUM_EXPERTS, D, 2 * D), jnp.float32) * s, 'b1': jnp.zeros((NUM_EXPERTS, 2 * D), jnp.float32), 'W2': jax.random.normal(ks[5], (NUM_EXPERTS, 2 * D, D), jnp.float32) * s, 'b2': jnp.zeros((NUM_EXPERTS, D), jnp.float32), 'edge_index': jax.random.randint(ks[6], (2, N_EDGES), 0, B * N, jnp.int32)}
    _L0_ffn_all = _L0_ffn_setup()
    _L0_ffn_in = {k: v for k, v in _L0_ffn_all.items() if k in ('W_gat', 'att_src', 'att_dst', 'b_gat', 'ln_gamma', 'ln_beta', 'W1', 'b1', 'W2', 'b2', 'edge_index')}
    del _L0_ffn_all
    return {'x': x, 'L0_conv_Wq': _L0_conv_in['Wq'], 'L0_conv_bq': _L0_conv_in['bq'], 'L0_conv_Wkv': _L0_conv_in['Wkv'], 'L0_conv_bkv': _L0_conv_in['bkv'], 'L0_conv_Wproj': _L0_conv_in['Wproj'], 'L0_conv_bproj': _L0_conv_in['bproj'], 'L0_conv_bias_table': _L0_conv_in['bias_table'], 'L0_ffn_W_gat': _L0_ffn_in['W_gat'], 'L0_ffn_att_src': _L0_ffn_in['att_src'], 'L0_ffn_att_dst': _L0_ffn_in['att_dst'], 'L0_ffn_b_gat': _L0_ffn_in['b_gat'], 'L0_ffn_ln_gamma': _L0_ffn_in['ln_gamma'], 'L0_ffn_ln_beta': _L0_ffn_in['ln_beta'], 'L0_ffn_W1': _L0_ffn_in['W1'], 'L0_ffn_b1': _L0_ffn_in['b1'], 'L0_ffn_W2': _L0_ffn_in['W2'], 'L0_ffn_b2': _L0_ffn_in['b2'], 'L0_ffn_edge_index': _L0_ffn_in['edge_index']}

def reference(x, L0_conv_Wq, L0_conv_bq, L0_conv_Wkv, L0_conv_bkv, L0_conv_Wproj, L0_conv_bproj, L0_conv_bias_table, L0_ffn_W_gat, L0_ffn_att_src, L0_ffn_att_dst, L0_ffn_b_gat, L0_ffn_ln_gamma, L0_ffn_ln_beta, L0_ffn_W1, L0_ffn_b1, L0_ffn_W2, L0_ffn_b2, L0_ffn_edge_index):
    import jax
    import jax.numpy as jnp

    def _L0_conv_ref(x, Wq, bq, Wkv, bkv, Wproj, bproj, bias_table):
        import jax, jax.numpy as jnp
        import numpy as np
        B, C, H, W = (2, 128, 128, 128)
        NH = 8
        DK = C // NH
        WS = 8
        SS = 4
        L = WS * WS
        NW = H // WS * (W // WS)

        def _relative_position_index(ws):
            coords = np.stack(np.meshgrid(np.arange(ws), np.arange(ws), indexing='ij'))
            cf = coords.reshape(2, -1)
            rel = cf[:, :, None] - cf[:, None, :]
            rel = rel.transpose(1, 2, 0).astype(np.int64)
            rel[..., 0] += ws - 1
            rel[..., 1] += ws - 1
            rel[..., 0] *= 2 * ws - 1
            return rel.sum(-1)

        def _shift_attn_mask(h, w, ws, ss):
            img = np.zeros((h, w), dtype=np.float32)
            slices = (slice(0, -ws), slice(-ws, -ss), slice(-ss, None))
            cnt = 0
            for hs in slices:
                for wsl in slices:
                    img[hs, wsl] = cnt
                    cnt += 1
            m = img.reshape(h // ws, ws, w // ws, ws).transpose(0, 2, 1, 3).reshape(-1, ws * ws)
            diff = m[:, None, :] - m[:, :, None]
            return np.where(diff != 0, -100.0, 0.0).astype(np.float32)
        _REL_IDX = jnp.asarray(_relative_position_index(WS).reshape(-1))
        _ATTN_MASK = jnp.asarray(_shift_attn_mask(H, W, WS, SS))

        def _partition(t):
            t = t.reshape(B, C, H // WS, WS, W // WS, WS)
            t = t.transpose(0, 2, 4, 1, 3, 5)
            return t.reshape(B * NW, NH, DK, L)
        q = jnp.einsum('oc,bchw->bohw', Wq, x) + bq[None, :, None, None]
        kv = jnp.einsum('oc,bchw->bohw', Wkv, x) + bkv[None, :, None, None]
        k, v = (kv[:, :C], kv[:, C:])
        q = jnp.roll(q, (-SS, -SS), axis=(2, 3))
        k = jnp.roll(k, (-SS, -SS), axis=(2, 3))
        v = jnp.roll(v, (-SS, -SS), axis=(2, 3))
        q, k, v = (_partition(q), _partition(k), _partition(v))
        attn = jnp.einsum('bhct,bhcs->bhts', q, k) * DK ** (-0.5)
        bias = bias_table[_REL_IDX].reshape(L, L, NH).transpose(2, 0, 1)
        attn = attn + bias[None]
        attn = attn.reshape(B, NW, NH, L, L) + _ATTN_MASK[None, :, None]
        attn = jax.nn.softmax(attn, axis=-1).reshape(B * NW, NH, L, L)
        out = jnp.einsum('bhts,bhcs->bhct', attn, v)
        out = out.reshape(B, H // WS, W // WS, C, WS, WS)
        out = out.transpose(0, 3, 1, 4, 2, 5).reshape(B, C, H, W)
        out = jnp.roll(out, (SS, SS), axis=(2, 3))
        out = jnp.einsum('oc,bchw->bohw', Wproj, out) + bproj[None, :, None, None]
        return out

    def _L0_ffn_ref(x, W_gat, att_src, att_dst, b_gat, ln_gamma, ln_beta, W1, b1, W2, b2, edge_index):
        import jax, jax.numpy as jnp
        import numpy as np
        B, N, D = (16, 2048, 128)
        NUM_EXPERTS, TOP_K, HEADS = (4, 2, 4)
        N_EDGES = 524288
        LN_EPS = 1e-05

        def _layernorm(x, g, b):
            mu = x.mean(-1, keepdims=True)
            var = ((x - mu) ** 2).mean(-1, keepdims=True)
            return (x - mu) * jax.lax.rsqrt(var + LN_EPS) * g + b

        def _forward(x, edge_index, W_gat, att_src, att_dst, b_gat, ln_gamma, ln_beta, W1, b1, W2, b2):
            Bc, Nc, Dc = x.shape
            M = Bc * Nc
            x_flat = x.reshape(M, Dc)
            h = (x_flat @ W_gat).reshape(M, HEADS, NUM_EXPERTS)
            loops = jnp.arange(M, dtype=edge_index.dtype)
            src = jnp.concatenate([edge_index[0], loops])
            dst = jnp.concatenate([edge_index[1], loops])
            a_src = (h * att_src).sum(-1)
            a_dst = (h * att_dst).sum(-1)
            e = jax.nn.leaky_relu(a_src[src] + a_dst[dst], negative_slope=0.2)
            e_max = jax.ops.segment_max(e, dst, num_segments=M)
            ee = jnp.exp(e - e_max[dst])
            denom = jax.ops.segment_sum(ee, dst, num_segments=M)
            alpha = ee / (denom[dst] + 1e-16)
            msg = h[src] * alpha[:, :, None]
            agg = jax.ops.segment_sum(msg, dst, num_segments=M).reshape(M, HEADS * NUM_EXPERTS) + b_gat
            scores = _layernorm(agg, ln_gamma, ln_beta).reshape(M, HEADS, NUM_EXPERTS).mean(1)
            scores = scores.reshape(Bc, Nc, NUM_EXPERTS)
            topk_s, topk_i = jax.lax.top_k(scores, TOP_K)
            w = jax.nn.softmax(topk_s, axis=-1)
            out = jnp.zeros_like(x)
            for ei in range(NUM_EXPERTS):
                g = jnp.where(topk_i == ei, w, 0.0).sum(-1)
                hh = jax.nn.gelu(x @ W1[ei] + b1[ei], approximate=False)
                out = out + g[..., None] * (hh @ W2[ei] + b2[ei])
            return out
        return _forward(x, edge_index, W_gat, att_src, att_dst, b_gat, ln_gamma, ln_beta, W1, b1, W2, b2)

    def _gn(v, G=32, eps=1e-05):
        B_, C_, H_, W_ = v.shape
        g = v.reshape(B_, G, C_ // G, H_, W_)
        m = jnp.mean(g, axis=(2, 3, 4), keepdims=True)
        s = jnp.var(g, axis=(2, 3, 4), keepdims=True)
        return ((g - m) / jnp.sqrt(s + eps)).reshape(v.shape)

    def _ln_c(v, eps=1e-06):
        m = jnp.mean(v, axis=1, keepdims=True)
        s = jnp.var(v, axis=1, keepdims=True)
        return (v - m) / jnp.sqrt(s + eps)

    def _ln_t(v, eps=1e-05):
        m = jnp.mean(v, axis=-1, keepdims=True)
        s = jnp.var(v, axis=-1, keepdims=True)
        return (v - m) / jnp.sqrt(s + eps)

    def _to_tokens(v):
        B_, C_, H_, W_ = v.shape
        return v.reshape(B_, C_, H_ * W_).transpose(0, 2, 1)

    def _from_tokens(t, like):
        B_, C_, H_, W_ = like.shape
        return t.transpose(0, 2, 1).reshape(B_, C_, H_, W_)
    x = x + _L0_conv_ref(_ln_c(x), L0_conv_Wq, L0_conv_bq, L0_conv_Wkv, L0_conv_bkv, L0_conv_Wproj, L0_conv_bproj, L0_conv_bias_table)
    t = _to_tokens(x)
    t = t + _L0_ffn_ref(_ln_t(t), L0_ffn_W_gat, L0_ffn_att_src, L0_ffn_att_dst, L0_ffn_b_gat, L0_ffn_ln_gamma, L0_ffn_ln_beta, L0_ffn_W1, L0_ffn_b1, L0_ffn_W2, L0_ffn_b2, L0_ffn_edge_index)
    x = _from_tokens(t, x)
    return x

_drawn_inputs = setup_inputs


def setup_inputs(seed=0):
    import zlib

    import numpy as np

    out = dict(_drawn_inputs(seed))
    spreads = {'L0_conv_bq': (0.0, 0.8),
     'L0_conv_bkv': (0.0, 0.1),
     'L0_conv_bproj': (0.0, 0.1),
     'L0_ffn_b_gat': (0.0, 0.1),
     'L0_ffn_ln_gamma': (1.0, 0.2),
     'L0_ffn_ln_beta': (0.0, 0.1),
     'L0_ffn_b1': (0.0, 0.1),
     'L0_ffn_b2': (0.0, 0.1)}
    factors = {'L0_conv_Wq': 8.0,
     'L0_conv_Wkv': 5.485,
     'L0_conv_bias_table': 26.543,
     'L0_ffn_att_dst': 11.813}
    for name, (base, spread) in spreads.items():
        noise = np.random.default_rng([zlib.crc32(name.encode()), seed]).standard_normal(out[name].shape)
        drawn = base * np.exp(spread * noise) if base else spread * noise
        out[name] = jnp.asarray(drawn.astype(out[name].dtype))
    for name, factor in factors.items():
        out[name] = (out[name] * factor).astype(out[name].dtype)
    return out
```

```python
from contextlib import ExitStack

import numpy as np

import concourse.bass as bass
from concourse import mybir

F32 = mybir.dt.float32
BF16 = mybir.dt.bfloat16
I32 = mybir.dt.int32
U32 = mybir.dt.uint32
ALU = mybir.AluOpType
ACT = mybir.ActivationFunctionType
AX = mybir.AxisListType.X

P = 128
C = 128
IMGS, H, W = 2, 128, 128
M = IMGS * H * W
NH, DK, WS, SS = 8, 16, 8, 4
L = WS * WS
NWIN = W // WS
STRIPS = IMGS * H // WS
STOK = WS * W
HTOK = STOK // 2
REL = (2 * WS - 1) ** 2
EDGES = 524288
EC = EDGES // P
TC = M // P
MERGED = EDGES + M
GH, NE = 4, 4
GC = GH * NE
ROW = GC + 2 * GH
FF = 256
SRC_BITS = 15
KEY_BASE = 256
U = 64
BIG = 1.0e30
LN_C_EPS, LN_T_EPS, GATE_EPS, DEN_EPS = 1e-6, 1e-5, 1e-5, 1e-16

CONST = {}
_at = 0
for _name, _n in (("ident", P), ("center", P), ("mean", P), ("upper", P), ("ones", P), ("even", 1), ("odd", 1),
                  ("sign", 7), ("iota", 256), ("shift_mask", 4 * L), ("row_base", 2), ("earlier", 16)):
    CONST[_name] = (_at, _at + _n)
    _at += _n
CONST_COLS = _at


def constants():
    c = np.zeros((P, CONST_COLS), np.float32)

    def put(name, value):
        a, b = CONST[name]
        c[:, a:b] = value

    p = np.arange(P)
    put("ident", np.eye(P))
    put("center", np.eye(P) - 1.0 / P)
    put("mean", np.full((P, P), 1.0 / P))
    put("upper", p[:, None] <= p[None, :])
    put("ones", 1.0)
    scale = DK ** -0.5
    put("even", np.where((p // DK) % 2 == 0, scale, 0.0)[:, None])
    put("odd", np.where((p // DK) % 2 == 1, scale, 0.0)[:, None])
    put("sign", np.where((p[:, None] >> np.arange(7)) & 1, -1.0, 1.0))
    put("iota", np.arange(256)[None, :])
    i, j = np.arange(L) // WS, np.arange(L) % WS
    masks = np.zeros((4, L, L), np.float32)
    for kind in range(4):
        region = (i >= WS - SS) * (2 * (kind // 2)) + (j >= WS - SS) * (kind % 2)
        masks[kind] = np.where(region[:, None] != region[None, :], -100.0, 0.0)
    put("shift_mask", np.tile(masks.transpose(1, 0, 2).reshape(L, 4 * L), (2, 1)))
    put("row_base", np.stack([p * EC - 1, EDGES + p * TC - 1], 1))
    put("earlier", (np.arange(NE)[None, :] < np.arange(NE)[:, None]).reshape(1, NE * NE))
    return c


def relative_one_hot():
    co = np.stack(np.meshgrid(np.arange(WS), np.arange(WS), indexing="ij")).reshape(2, -1)
    rel = co[:, :, None] - co[:, None, :] + (WS - 1)
    idx = rel[0] * (2 * WS - 1) + rel[1]
    out = np.zeros((REL, L, L), np.float32)
    t, s = np.meshgrid(np.arange(L), np.arange(L), indexing="ij")
    out[idx[t, s], s, t] = 1.0
    return out.reshape(REL, L * L)


N_LOADS = 20
OPEN = 2


class Done:

    def __init__(self, eng, semaphore, start=0):
        self.eng, self.sem, self.n = eng, semaphore, start

    def step(self, ins):
        ins.then_inc(self.sem, 1)
        self.n += 1

    def settle(self):
        self.eng.wait_ge(self.sem, self.n)


def program(nc, x, wq_t, bq, wkv_t, bkv, wproj_t, bproj, bias_table, w_gat, att_src, att_dst, b_gat, ln_gamma,
            ln_beta, w1, b1, w2, b2, edges, const, rel_hot, out):
    node_rows = nc.dram_tensor("node_rows", (M, ROW), F32, kind="Internal").ap()
    edge_rows = nc.dram_tensor("edge_rows", (MERGED, ROW), F32, kind="Internal").ap()
    x1_dram = nc.dram_tensor("x1_dram", (C, M), F32, kind="Internal").ap()
    xn_dram = nc.dram_tensor("xn_dram", (C, M), F32, kind="Internal").ap()
    y_dram = nc.dram_tensor("y_dram", (M // P, P, NE * C), F32, kind="Internal").ap()

    with ExitStack() as ctx:
        scopes = [ctx]

        def sb(name, shape, dt=F32):
            return scopes[-1].enter_context(nc.sbuf_tensor(name, shape, dt))

        def sem(name):
            return ctx.enter_context(nc.semaphore(name))

        bank = ctx.enter_context(nc.psum_tensor("bank", [P, 8, 512], F32))
        cst = sb("cst", [P, CONST_COLS])

        def con(name):
            return cst[:, CONST[name][0]:CONST[name][1]]

        keys = [sb("key_a", [P, EC + TC]), sb("key_b", [P, EC + TC])]
        dst_f = sb("dst_f", [P, EC + TC + 2])
        vec = sb("vec", [C, 8])
        att_s = sb("att_s", [P, 2 * GC])
        gate_s = sb("gate_s", [P, 3 * GC])
        eps = sb("eps", [P, 2])
        wgat_s = sb("wgat_s", [C, GC])

        loaded = sem("loaded")
        vec_sums = sem("vec_sums")
        self_loops = sem("self_loops")
        key_step = sem("key_step")
        turned = sem("turned")
        turned_copy = sem("turned_copy")
        sorted_ = sem("sorted")

        evac = [sem(f"evac{b}") for b in range(2)]
        full = [sem(f"full{b}") for b in range(2)]
        x_loaded = [sem(f"x_loaded{b}") for b in range(2)]
        rstd_ready = sem("rstd_ready")
        xn_done = sem("xn_done")
        s_full = sem("s_full")
        biased = sem("biased")
        max_ready = sem("max_ready")
        centered = sem("centered")
        exp_ready = sem("exp_ready")
        inv_ready = sem("inv_ready")
        probs_ready = sem("probs_ready")
        pt_full = [sem(f"pt_full{b}") for b in range(2)]
        pt_evac = [sem(f"pt_evac{b}") for b in range(2)]
        strip_stored = [sem(f"strip_stored{b}") for b in range(2)]
        strip_saved = sem("strip_saved")
        dve_own = sem("dve_own")


        vb_zero = sem("vb_zero")
        join_step = sem("join_step")
        chunk_step = sem("chunk_step")
        hot_ready = sem("hot_ready")
        counted = sem("counted")
        count_added = sem("count_added")
        y_full = [sem(f"y_full{b}") for b in range(2)]
        y_evac = [sem(f"y_evac{b}") for b in range(2)]
        y_stored = sem("y_stored")
        y_saved = sem("y_saved")
        up_full = sem("up_full")
        hidden = sem("hidden")
        first_got = sem("first_got")
        idx_ready = sem("idx_ready")
        gathered = [sem(f"gathered{b}") for b in range(2)]
        diff_ready = sem("diff_ready")
        weights_ready = sem("weights_ready")
        edge_used = sem("edge_used")
        rows_done = sem("rows_done")
        rows_stored = sem("rows_stored")
        rows_saved = sem("rows_saved")
        experts_loaded = sem("experts_loaded")
        xm_loaded = [sem(f"xm_loaded{b}") for b in range(2)]
        prefix_full = sem("prefix_full")
        chain_ready = sem("chain_ready")
        chain_turned = sem("chain_turned")
        chain_diff = sem("chain_diff")
        chain_exp = sem("chain_exp")
        run_got = sem("run_got")
        runs_joined = sem("runs_joined")
        run_put = sem("run_put")
        got_landed = [sem(f"got_landed{b}") for b in range(2)]
        idx_d_ready = sem("idx_d_ready")
        idx_taken = sem("idx_taken")
        gate_step = sem("gate_step")
        gate_asks = sem("gate_asks")
        gate_asks2 = sem("gate_asks2")
        gate_std = sem("gate_std")
        gate_exp = sem("gate_exp")
        gates_ready = sem("gates_ready")
        yo_loaded = [sem(f"yo_loaded{b}") for b in range(2)]
        res_loaded = [sem(f"res_loaded{b}") for b in range(2)]
        mix_ready = sem("mix_ready")
        mix_turned = sem("mix_turned")
        fin_ready = sem("fin_ready")
        fin_saved = sem("fin_saved")
        out_stored = [sem(f"out_stored{b}") for b in range(2)]

        scratch_i = sb("scratch_i", [P, 2 * (EC + TC)], I32)
        edge_i = scratch_i[:, 0:2 * EC].rearrange("p (a f) -> p a f", a=2)
        run_flag = scratch_i[:, 0:EC].bitcast(F32)
        first_row_i = sb("first_row_i", [P, 2], I32)
        end_i = sb("end_i", [P, 256], I32)
        bias = sb("bias", [P, 4, NH // 2, L])
        wq_s = sb("wq_s", [C, C])
        wkv_s = sb("wkv_s", [C, 2 * C])
        wproj_s = sb("wproj_s", [C, C])
        loops_i = sb("loops_i", [P, 2, 32, 8], I32)
        tails = [sb("tail_a", [P, 256]), sb("tail_b", [P, 256])]

        setup = ExitStack()
        scopes.append(setup)
        hot = sb("hot", [P, 2, L * L])
        table_s = sb("table_s", [P, 2, NH])
        scopes.pop()
        setup.close()

        stage_b = ExitStack()
        scopes.append(stage_b)
        prob = [sb(f"prob{g}", [P, 8, NH // 2, L]) for g in range(2)]
        pt = sb("pt", [P, 8, 2, P])
        vb = sb("vb", [P, NWIN, 2, 2, L])
        xt = [sb(f"xt{b}", [C, WS, W]) for b in range(2)]
        xc = sb("xc", [C, 2, HTOK])
        sq = sb("sq", [C, 2, HTOK])
        std = sb("std", [C, 2, HTOK])
        rstd = sb("rstd", [C, 2, HTOK])
        xw = sb("xw", [C, NWIN, WS, WS])
        q2 = sb("q2", [C, NWIN, 2, L])
        kt = sb("kt", [C, NWIN, L])
        row_max = sb("row_max", [P, 2, 8, NH // 2])
        row_sum = sb("row_sum", [P, 2, 8, NH // 2])
        row_inv = sb("row_inv", [P, 2, 8, NH // 2])
        ot = sb("ot", [C, NWIN, WS, WS])
        x1 = [sb(f"x1{b}", [C, WS, W]) for b in range(2)]
        x2 = [sb(f"x2{b}", [C, WS, W]) for b in range(2)]
        node = [sb(f"node{b}", [P, WS, ROW]) for b in range(2)]
        node_att = sb("node_att", [P, 2, 4, 2 * GC])
        scopes.pop()
        stage_b.close()

        stage_c = ExitStack()
        scopes.append(stage_c)
        gath = [sb(f"gath{b}", [P, U, ROW]) for b in range(2)]
        idx = [sb(f"idx{b}", [P, U], I32) for b in range(2)]
        hilo_i = sb("hilo_i", [P, 2, U], I32)
        hilo = sb("hilo", [P, 2, U])
        iota_b = sb("iota_b", [P, 256], BF16)
        hot_b = [sb(f"hot_b{b}", [P, 8, 384], BF16) for b in range(2)]
        count = sb("count", [P, 256])
        new4 = sb("new4", [P, GH, U])
        keep4 = sb("keep4", [P, GH, U + 1])
        mask4 = sb("mask4", [P, GH, U + 1])
        adst_in = sb("adst_in", [P, GH, U + 1])
        adst = sb("adst", [P, GH, U + 1])
        logit = sb("logit", [P, GH, U + 1])
        leaky = sb("leaky", [P, GH, U + 1])
        run_max = sb("run_max", [P, GH, U + 1])
        diff = sb("diff", [P, 2, GH, U + 1])
        weight = sb("weight", [P, 2, GH, U + 1])
        terms = sb("terms", [P, NE, GH, U + 1])
        sums = sb("sums", [P, 1 + NE, GH, U + 1])
        first = [sb(f"first{n}", [P, ROW]) for n in range(2)]
        rows = [sb(f"rows{b}", [P, U, ROW]) for b in range(2)]
        ends = sb("ends", [P, 2, ROW])
        w1_s = sb("w1_s", [C, NE, FF])
        w2_s = sb("w2_s", [P, NE, 2, C])
        b1_s = sb("b1_s", [P, NE, 2])
        b2_s = sb("b2_s", [P, NE, C])
        xm = [sb(f"xm{b}", [C, 512]) for b in range(2)]
        hid = scratch_i[:, EC + TC:EC + TC + NE * 2 * 512].bitcast(F32).rearrange("p (k t) -> p k t", t=512)
        yt = [scratch_i[:, 2048 * b:2048 * b + 2048].bitcast(F32).rearrange("p (t f) -> p t f", t=4)
              for b in range(2)]
        run_len = sb("run_len", [P, 2])
        row_i = sb("row_i", [P, 2], I32)
        chain_in = sb("chain_in", [P, 2, 4, 20])
        chain = sb("chain", [20, 4, 257])
        ck = sb("ck", [20, 6, 257])
        joined = sb("joined", [20, 2, 256])
        carry = sb("carry", [P, 2, 2, 20])
        at_run = sb("at_run", [P, 2, ROW])
        jw = sb("jw", [P, 3, 2, 4])
        end_f = sb("end_f", [P, 256])
        tot = sb("tot", [P, 2, 256])
        scopes.pop()
        stage_c.close()

        stage_d = ExitStack()
        scopes.append(stage_d)
        idx_d = [sb(f"idx_d{b}", [P, 32], I32) for b in range(2)]
        got = [sb(f"got{b}", [P, 32, ROW]) for b in range(2)]
        sc = sb("sc", [P, 4, 32, GC])
        s1 = sb("s1", [P, 8, 32])
        s4 = sb("s4", [P, 6, 32, NE])
        gates = [sb(f"gates{b}", [P, 32, NE]) for b in range(2)]
        mix = [sb(f"mix{b}", [P, 4, C]) for b in range(2)]
        res = [sb(f"res{b}", [C, 512]) for b in range(2)]
        yo = [sb(f"yo{b}", [P, 4, NE * C]) for b in range(2)]
        fin = [sb(f"fin{b}", [C, 512]) for b in range(2)]
        scopes.pop()
        stage_d.close()

        block = ctx.enter_context(nc.Block())
        marks = {}

        def key(k):
            return keys[k][:, 0:EC]

        def exchange(d, src, dst, dist, blk):
            e = d.eng
            d.settle()
            if blk is None:
                s = src.rearrange("p (b t i) -> p b t i", t=2, i=dist)
                o = dst.rearrange("p (b t i) -> p b t i", t=2, i=dist)
                pairs = [(s[:, :, 0], s[:, :, 1], o[:, :, 0], o[:, :, 1])]
            else:
                n = blk // (2 * dist)
                s = src.rearrange("p (b r s t i) -> p r t b s i", r=2, t=2, i=dist, s=n)
                o = dst.rearrange("p (b r s t i) -> p r t b s i", r=2, t=2, i=dist, s=n)
                pairs = [(s[:, 0, 0], s[:, 0, 1], o[:, 0, 0], o[:, 0, 1]),
                         (s[:, 1, 0], s[:, 1, 1], o[:, 1, 1], o[:, 1, 0])]
            for lower, upper, small, large in pairs:
                d.step(e.tensor_tensor(small, lower, upper, ALU.min))
                d.step(e.tensor_tensor(large, lower, upper, ALU.max))

        def dve_setup(d):
            e = d.eng
            e.wait_ge(loaded, 16 * N_LOADS)
            d.step(e.memset(eps[:, 0:1], LN_C_EPS))
            d.step(e.memset(eps[:, 1:2], LN_T_EPS))
            d.step(e.tensor_scalar(vec[:, 4:5], vec[:, 0:1], con("even"), None, ALU.mult))
            d.step(e.tensor_scalar(vec[:, 5:6], vec[:, 0:1], con("odd"), None, ALU.mult))
            e.wait_ge(vec_sums, 2)
            d.step(e.tensor_tensor(vec[:, 6:7], bank[:, 1, 0:1], vec[:, 3:4], ALU.add))
            table = bank[:, 0, :].rearrange("p (s h) -> p h s", h=NH)
            mask = con("shift_mask").rearrange("p (k s) -> p k s", k=4)
            for half in range(2):
                rws = slice(64 * half, 64 * half + 64)
                for kind in range(4):
                    d.step(e.tensor_tensor(bias[rws, kind], table[rws, half::2, :],
                                           mask[rws, kind:kind + 1, :].broadcast_to([64, NH // 2, L]), ALU.add))

        def dve_sort(d):
            e = d.eng
            xor = keys[1][:, 0:EC].bitcast(I32)
            base = keys[0][:, 0:EC].bitcast(I32)
            d.step(e.tensor_tensor(xor, edge_i[:, 0, :], edge_i[:, 1, :], ALU.bitwise_xor))
            d.step(e.tensor_scalar(base, edge_i[:, 1, :], float(KEY_BASE), None, ALU.add))
            d.settle()
            d.step(e.scalar_tensor_tensor(edge_i[:, 0, :], base, SRC_BITS, xor, ALU.logical_shift_left,
                                          ALU.bitwise_or))
            e.wait_ge(self_loops, 1)
            d.step(e.tensor_scalar(loops_i[:, 1], loops_i[:, 0], SRC_BITS, None, ALU.logical_shift_left))
            d.settle()
            d.step(e.tensor_scalar(key(0), edge_i[:, 0, :].bitcast(F32), con("sign")[:, 0:1], None, ALU.mult))
            cur = 0
            blk = 2
            while blk <= EC:
                dist = blk // 2
                while dist:
                    exchange(d, key(cur), key(1 - cur), dist, None if blk == EC else blk)
                    cur = 1 - cur
                    dist //= 2
                blk *= 2
            for level in range(1, 9):
                marks["across", level] = (d.n, cur)
                e.wait_ge(turned_copy, 16 * level - 8)
                cur = 1 - cur
                dist = P // 2
                blk = None
                if level < 8:
                    dist = 1 << (level - 1)
                    blk = None if level == 7 else 2 * dist
                    s, o = key(cur), key(1 - cur)
                    if blk is None:
                        s = s.rearrange("p (b t i) -> p b t i", t=2, i=dist)
                        o = o.rearrange("p (b t i) -> p b t i", t=2, i=dist)
                        pairs = [(s[:, :, 0], s[:, :, 1], o[:, :, 0], o[:, :, 1])]
                    else:
                        s = s.rearrange("p (b r t i) -> p r t b i", r=2, t=2, i=dist)
                        o = o.rearrange("p (b r t i) -> p r t b i", r=2, t=2, i=dist)
                        pairs = [(s[:, 0, 0], s[:, 0, 1], o[:, 0, 0], o[:, 0, 1]),
                                 (s[:, 1, 0], s[:, 1, 1], o[:, 1, 1], o[:, 1, 0])]
                    for lower, upper, small, large in pairs:
                        d.step(e.scalar_tensor_tensor(small, upper, -1.0, lower, ALU.mult, ALU.min))
                        d.step(e.scalar_tensor_tensor(large, upper, -1.0, lower, ALU.mult, ALU.max))
                    cur = 1 - cur
                    dist //= 2
                else:
                    last = key(cur).rearrange("p (h b q) -> p h b q", b=2, q=P)[:, :, :, P - 8:P]
                    loops = loops_i[:, 1].bitcast(F32).rearrange("p (h b) q -> p h b q", b=2)
                    large, small = (t[:, :].rearrange("p (b q h) -> p h b q", b=2, q=8) for t in tails)
                    d.step(e.tensor_tensor(large, last, loops, ALU.max))
                    d.step(e.tensor_tensor(small, last, loops, ALU.min))
                    d.settle()
                    d.step(e.tensor_copy(last, small))
                while dist:
                    exchange(d, key(cur), key(1 - cur), dist, blk)
                    cur = 1 - cur
                    dist //= 2
                if level == 8:
                    for n, dist in enumerate((64, 32, 16, 8, 4, 2, 1, 128)):
                        exchange(d, tails[n % 2][:, :], tails[1 - n % 2][:, :], dist, None)
                marks["back", level] = (d.n, cur)
                e.wait_ge(turned_copy, 16 * level)
                cur = 1 - cur
                dist = EC // 2
                while dist:
                    exchange(d, key(cur), key(1 - cur), dist, None)
                    cur = 1 - cur
                    dist //= 2
            e.wait_ge(turned_copy, 16 * 8 + 1)
            for n in range(7):
                exchange(d, tails[1 - n % 2][:, :], tails[n % 2][:, :], P // 2 >> n, None)
            d.settle()
            d.step(e.tensor_copy(keys[cur][:, EC:], tails[0][:, :]))
            k = keys[cur][:, :].bitcast(I32)
            src = keys[1 - cur][:, :].bitcast(I32)
            raw, dst_i = scratch_i[:, 0:EC + TC], scratch_i[:, EC + TC:]
            d.settle()
            d.step(e.tensor_scalar(raw, k, SRC_BITS, None, ALU.logical_shift_right))
            d.settle()
            d.step(e.tensor_scalar(dst_i, raw, -float(KEY_BASE), None, ALU.add))
            d.settle()
            d.step(e.scalar_tensor_tensor(src, k, (1 << SRC_BITS) - 1, dst_i, ALU.bitwise_and, ALU.bitwise_xor))
            d.step(e.tensor_copy(dst_f[:, 1:1 + EC], dst_i[:, 0:EC]))
            d.step(e.tensor_copy(dst_f[:, 2 + EC:], dst_i[:, EC:]))
            d.settle()
            d.step(e.tensor_copy(dst_f[:, 0:1], dst_f[:, 1:2]))
            d.step(e.tensor_copy(dst_f[:, 1 + EC:2 + EC], dst_f[:, 2 + EC:3 + EC]))
            d.step(e.tensor_copy(first_row_i[:, 0:1], dst_i[:, 0:1]))
            d.step(e.tensor_copy(first_row_i[:, 1:2], dst_i[:, EC:EC + 1]))
            d.settle()
            e.sem_inc(sorted_, 1)
            marks["sorted"] = (d.n, cur)

        n_rstd = 4

        def strip_dve(e, s, par, last):
            def inverse_std(n):
                for j in range(2):
                    wait_evac(e, s, (2, 18)[n] + j)
                    e.wait_ge(xn_done, s * 4 + 2 * n + OPEN)
                    e.reciprocal(rstd[:, j], std[:, j]).then_inc(rstd_ready, 1)

            def add_bias(g):
                e.wait_ge(s_full, s * 2 + g + 1 + OPEN)
                e.wait_ge(pt_full[1], s * 4 + OPEN)
                kind = bias[:, bass.ds(last * 2, 1)] if not isinstance(last, int) else bias[:, 2 * last:2 * last + 1]
                edge = bias[:, bass.ds(last * 2 + 1, 1)] if not isinstance(last, int) else \
                    bias[:, 2 * last + 1:2 * last + 2]
                scores = bank[:, 0:4, :].rearrange("p h (w s) -> p h w s", s=L)
                n = 8 - g
                taken = prob[g][:, :, :, :].rearrange("p w h s -> p h w s")
                e.tensor_tensor(taken[:, :, 0:n], scores[:, :, 0:n],
                                kind.rearrange("p k h s -> p h k s").broadcast_to([P, NH // 2, n, L]),
                                ALU.add).then_inc(biased, 1)
                if g:
                    e.tensor_tensor(taken[:, :, n:8], scores[:, :, n:8],
                                    edge.rearrange("p k h s -> p h k s"), ALU.add).then_inc(biased, 1)
                e.wait_ge(biased, s * 3 + 1 + 2 * g + OPEN)
                e.tensor_reduce(row_max[:, g], prob[g][:, :, :, :], AX, ALU.max).then_inc(max_ready, 1)

            def inverse_sum(g):
                e.wait_ge(exp_ready, s * 2 + g + 1 + OPEN)
                e.tensor_reduce(row_sum[:, g], prob[g][:, :, :, :], AX, ALU.add).then_inc(dve_own, 1)
                e.wait_ge(dve_own, s * 6 + g + 1 + OPEN)
                e.reciprocal(row_inv[:, g], row_sum[:, g]).then_inc(inv_ready, 1)

            inverse_std(0)
            add_bias(0)
            add_bias(1)
            inverse_sum(0)
            inverse_sum(1)
            for j in range(2):
                wait_full(e, s, 14 + j)
                e.wait_ge(strip_saved, s - 1 + OPEN)
                pr = bank[:, 6 + j, :].rearrange("p (i c) -> p i c", c=W)
                rws = slice(4 * j, 4 * j + 4)
                e.scalar_tensor_tensor(x1[par][:, rws, SS:W], pr[:, :, 0:W - SS], vec[:, 6:7],
                                       xt[par][:, rws, SS:W], ALU.add, ALU.add)
                e.scalar_tensor_tensor(x1[par][:, rws, 0:SS], pr[:, :, W - SS:W], vec[:, 6:7],
                                       xt[par][:, rws, 0:SS], ALU.add, ALU.add).then_inc(evac[j], 1)
            inverse_std(1)
            for j in range(2):
                wait_full(e, s, 20 + j)
                nd = node[par][:, 4 * j:4 * j + 4, :]
                e.tensor_copy(nd[:, :, 0:GC],
                              bank[:, 6 + j, 0:4 * GC].rearrange("p (r c) -> p r c", c=GC)).then_inc(evac[j], 1)
                e.wait_ge(evac[j], s * 11 + 11 + OPEN)
                e.tensor_tensor(node_att[:, j].rearrange("p r (k c) -> p r k c", k=2),
                                nd[:, :, 0:GC].unsqueeze(2).broadcast_to([P, 4, 2, GC]),
                                att_s[:, :].rearrange("p (k c) -> p k c", k=2).unsqueeze(1)
                                .broadcast_to([P, 4, 2, GC]), ALU.mult).then_inc(dve_own, 1)
                e.wait_ge(dve_own, s * 6 + 3 + 2 * j + OPEN)
                e.tensor_reduce(nd[:, :, GC:ROW],
                                node_att[:, j].rearrange("p r (h e) -> p r h e", e=NE), AX,
                                ALU.add).then_inc(dve_own, 1)

        def wait_evac(e, s, u):
            e.wait_ge(evac[u % 2], s * 11 + u // 2 + 1 + OPEN)

        def wait_full(e, s, u):
            e.wait_ge(full[u % 2], s * 11 + u // 2 + 1 + OPEN)

        def pe_setup(e):
            e.wait_ge(loaded, 16 * N_LOADS)
            rest = REL - P
            for s in range(L):
                for half in range(2):
                    for n, rws in enumerate((P, rest)):
                        last = e.matmul(bank[L * half:L * half + L, 0, NH * s:NH * s + NH],
                                        hot[0:rws, n, L * s:L * s + L], table_s[0:rws, n, :],
                                        start=n == 0, stop=n == 1)
            last.then_inc(vec_sums, 1)
            e.matmul(bank[:, 1, 0:1], wproj_s[:, :], vec[:, 2:3], start=True, stop=True).then_inc(vec_sums, 1)

        def pe_sort(e):
            for level in range(1, 9):
                for way, done in (("across", 0), ("back", 8)):
                    n, cur = marks[way, level]
                    e.wait_ge(key_step, n)
                    for k in range(8):
                        if level > 1 or done:
                            e.wait_ge(turned_copy, 16 * (level - 1) + done - 8 + k + 1)
                        for q in range(4):
                            part = slice(P * (4 * k + q), P * (4 * k + q) + P)
                            t = e.transpose(bank[:, k, P * q:P * q + P], key(cur)[:, part], con("ident"))
                        t.then_inc(turned, 1)
            e.wait_ge(turned_copy, 16 * 8)
            for b in range(2):
                t = e.transpose(bank[:, 0, P * b:P * b + P],
                                tails[0][:, P * b:P * b + P], con("ident"))
            t.then_inc(turned, 1)

        def strip_pe(e, s, par, i):
            def free(u):
                e.wait_ge(evac[u % 2], s * 11 + u // 2 + OPEN)

            def bk(u):
                return bank[:, 6 + u % 2, :]

            def layernorm(u0, source, loaded_wait):
                for j in range(2):
                    free(u0 + j)
                    loaded_wait(j)
                    e.matmul(bk(u0 + j), con("center"), source[:, 4 * j:4 * j + 4, :].rearrange("c i w -> c (i w)"),
                             start=True, stop=True).then_inc(full[j], 1)
                for j in range(2):
                    free(u0 + 2 + j)
                    e.matmul(bk(u0 + 2 + j), con("mean"), sq[:, j], start=True, stop=True).then_inc(full[j], 1)

            layernorm(0, xt[par], lambda j: e.wait_ge(x_loaded[par], 32 * (i + 1)))
            e.wait_ge(xn_done, s * 4 + 2 + OPEN)
            for g in range(2):
                wins = xw[:, 8 * g:8 * g + 8].rearrange("c w i j -> c (w i j)")
                for n, wgt in enumerate((wq_s[:, :], wkv_s[:, 0:C])):
                    free(4 + 4 * g + n)
                    e.matmul(bk(n), wgt, wins, start=True, stop=True).then_inc(full[n], 1)
                for n in range(2):
                    free(6 + 4 * g + n)
                    for w in range(4):
                        win = xw[:, 8 * g + 4 * n + w].rearrange("c i j -> c (i j)")
                        for k in range(2):
                            m = e.matmul(bk(n)[L * k:L * k + L, L * w:L * w + L], win,
                                         wkv_s[:, C:2 * C].rearrange("c (u k d) -> c k u d", k=2, d=2 * DK)[:, k],
                                         start=True, stop=True)
                    m.then_inc(full[n], 1)
            for g in range(2):
                wait_evac(e, s, 4 + 4 * g)
                wait_evac(e, s, 5 + 4 * g)
                e.wait_ge(biased, s * 3 + g + OPEN)
                for w in range(8):
                    for h in range(NH // 2):
                        rws = slice(32 * h, 32 * h + 32)
                        m = e.matmul(bank[:, h, L * w:L * w + L], q2[rws, 8 * g + w].rearrange("c v t -> c (v t)"),
                                     kt[rws, 8 * g + w], start=True, stop=True)
                m.then_inc(s_full, 1)
            for g in range(2):
                e.wait_ge(probs_ready, s * 2 + g + 1 + OPEN)
                for wp in range(4):
                    b = wp % 2
                    e.wait_ge(pt_evac[b], s * 4 + 2 * g + wp // 2 + OPEN)
                    for w in range(2):
                        for hh in range(2):
                            t = e.transpose(bank[:, 4 + b, P * (2 * w + hh):P * (2 * w + hh) + P],
                                            prob[g][:, 2 * wp + w, 2 * hh:2 * hh + 2, :].rearrange("p k s -> p (k s)"), con("ident"))
                    t.then_inc(pt_full[b], 1)
                for b in range(2):
                    e.wait_ge(pt_evac[b], s * 4 + 2 * g + 2 + OPEN)
                    wait_evac(e, s, 6 + 4 * g + b)
                free(12 + g)
                for w in range(8):
                    for hh in range(2):
                        for v in range(2):
                            m = e.matmul(bank[64 * hh:64 * hh + 64, 6 + g, L * w:L * w + L],
                                         vb[:, 8 * g + w, hh, v, :], pt[:, w, hh, 64 * v:64 * v + 64],
                                         start=v == 0, stop=v == 1)
                m.then_inc(full[g], 1)
            wait_evac(e, s, 12)
            wait_evac(e, s, 13)
            for j in range(2):
                free(14 + j)
                e.matmul(bk(14 + j), wproj_s[:, :],
                         ot[:, :, 4 * j:4 * j + 4, :].rearrange("c w i j -> c i w j"),
                         start=True, stop=True).then_inc(full[j], 1)
            layernorm(16, x1[par], lambda j: wait_evac(e, s, 14 + j))
            for j in range(2):
                e.wait_ge(xn_done, s * 4 + 3 + j + OPEN)
                free(20 + j)
                for r in range(4):
                    m = e.matmul(bank[:, 6 + j, GC * r:GC * r + GC], x2[par][:, 4 * j + r, :], wgat_s[:, :],
                                 start=True, stop=True)
                m.then_inc(full[j], 1)

        def act_sort(e):
            n = 0
            for level in range(1, 9):
                for way in ("across", "back"):
                    cur = marks[way, level][1]
                    for k in range(8):
                        n += 1
                        e.wait_ge(turned, n)
                        if way == "across" or level > 6:
                            e.activation(key(1 - cur)[:, 512 * k:512 * k + 512], bank[:, k, :],
                                         ACT.Copy).then_inc(turned_copy, 1)
                        else:
                            e.activation(key(1 - cur)[:, 512 * k:512 * k + 512], bank[:, k, :], ACT.Copy,
                                         scale=con("sign")[:, level:level + 1]).then_inc(turned_copy, 1)
            e.wait_ge(turned, n + 1)
            e.activation(tails[1][:, :], bank[:, 0, 0:256], ACT.Copy).then_inc(turned_copy, 1)

        def strip_act(e, s, par):
            def centered_copy(u0, n):
                for j in range(2):
                    wait_full(e, s, u0 + j)
                    e.wait_ge(xn_done, s * 4 + 2 * n + OPEN)
                    e.activation(xc[:, j], bank[:, 6 + j, :], ACT.Copy)
                    e.activation(sq[:, j], bank[:, 6 + j, :], ACT.Square).then_inc(evac[j], 1)
                for j in range(2):
                    wait_full(e, s, u0 + 2 + j)
                    e.wait_ge(rstd_ready, s * 4 + 2 * n + OPEN)
                    e.activation(std[:, j], bank[:, 6 + j, :], ACT.Sqrt,
                                 bias=eps[:, n:n + 1]).then_inc(evac[j], 1)

            centered_copy(0, 0)
            for g in range(2):
                wins = slice(8 * g, 8 * g + 8)
                wait_full(e, s, 4 + 4 * g)
                src = bank[:, 6, :].rearrange("p (w t) -> p w t", t=L)
                e.wait_ge(s_full, s * 2 + OPEN)
                e.activation(q2[:, wins, 0, :], src, ACT.Identity, bias=vec[:, 4:5], scale=con("even"))
                e.activation(q2[:, wins, 1, :], src, ACT.Identity, bias=vec[:, 5:6],
                             scale=con("odd")).then_inc(evac[0], 1)
                wait_full(e, s, 5 + 4 * g)
                e.activation(kt[:, wins, :], bank[:, 7, :].rearrange("p (w t) -> p w t", t=L), ACT.Identity,
                             bias=vec[:, 1:2]).then_inc(evac[1], 1)
                for n in range(2):
                    wait_full(e, s, 6 + 4 * g + n)
                    for half in range(2):
                        rws = slice(64 * half, 64 * half + 64)
                        src = bank[rws, 6 + n, 0:4 * L].rearrange("p (w v d) -> p v w d", v=2, d=DK)
                        for v in range(2):
                            dst = vb[rws, 8 * g + 4 * n:8 * g + 4 * n + 4, :, v, :].rearrange(
                                "p w h (k u d) -> p k u (w h) d", k=2, u=2)
                            a = e.activation(dst[:, half, v], src[:, v], ACT.Copy)
                    a.then_inc(evac[n], 1)
            for g in range(2):
                e.wait_ge(centered, s * 2 + g + 1 + OPEN)
                e.activation(prob[g][:, :, :, :], prob[g][:, :, :, :], ACT.Exp).then_inc(exp_ready, 1)
            for g in range(2):
                for wp in range(4):
                    b = wp % 2
                    e.wait_ge(pt_full[b], s * 4 + 2 * g + wp // 2 + 1 + OPEN)
                    if wp == 0 and g == 1:
                        wait_full(e, s, 12)
                    e.activation(pt[:, 2 * wp:2 * wp + 2], bank[:, 4 + b, :].rearrange(
                        "p (w h t) -> p w h t", w=2, h=2), ACT.Copy).then_inc(pt_evac[b], 1)
                wait_full(e, s, 12 + g)
                e.activation(ot[:, 8 * g:8 * g + 8], bank[:, 6 + g, :].rearrange(
                    "p (w i j) -> p w i j", i=WS, j=WS), ACT.Copy).then_inc(evac[g], 1)
            centered_copy(16, 1)

        def strip_pool(e, s, par):
            for j in range(2):
                e.wait_ge(rstd_ready, s * 4 + j + 1 + OPEN)
                e.wait_ge(full[1], s * 11 + OPEN)
                a = xc[:, j].rearrange("c (i w) -> c i w", w=W)
                r = rstd[:, j].rearrange("c (i w) -> c i w", w=W)
                o = xw[:, :, 4 * j:4 * j + 4, :].rearrange("c w i j -> c i w j")
                mid = slice(SS, SS + (NWIN - 1) * WS)
                e.tensor_tensor(o[:, :, 0:NWIN - 1, :], a[:, :, mid].rearrange("c i (w j) -> c i w j", j=WS),
                                r[:, :, mid].rearrange("c i (w j) -> c i w j", j=WS), ALU.mult)
                e.tensor_tensor(o[:, :, NWIN - 1, 0:SS], a[:, :, W - SS:W], r[:, :, W - SS:W], ALU.mult)
                e.tensor_tensor(o[:, :, NWIN - 1, SS:WS], a[:, :, 0:SS], r[:, :, 0:SS],
                                ALU.mult).then_inc(xn_done, 1)
            for g in range(2):
                e.wait_ge(max_ready, s * 2 + g + 1 + OPEN)
                pr = prob[g][:, :, :, :].rearrange("p w h s -> p (w h) s")
                e.tensor_tensor(pr, pr, row_max[:, g].rearrange("p w h -> p (w h)").unsqueeze(2)
                                .broadcast_to([P, 32, L]), ALU.subtract).then_inc(centered, 1)
            for g in range(2):
                e.wait_ge(inv_ready, s * 2 + g + 1 + OPEN)
                pr = prob[g][:, :, :, :].rearrange("p w h s -> p (w h) s")
                e.tensor_tensor(pr, pr, row_inv[:, g].rearrange("p w h -> p (w h)").unsqueeze(2)
                                .broadcast_to([P, 32, L]), ALU.mult).then_inc(probs_ready, 1)
            for j in range(2):
                e.wait_ge(rstd_ready, s * 4 + 3 + j + OPEN)
                e.wait_ge(strip_saved, s - 1 + OPEN)
                e.tensor_tensor(x2[par][:, 4 * j:4 * j + 4, :].rearrange("c i w -> c (i w)"), xc[:, j], rstd[:, j],
                                ALU.mult).then_inc(xn_done, 1)

        EPIECE = EC // U
        TPIECE = TC // U

        def piece_start(d, n):
            e = d.eng
            if n == 0:
                e.wait_ge(first_got, 32)
                for t in (keep4[:, :, 0:1], weight[:, 0, :, 0:1]):
                    d.step(e.memset(t, 0.0))
                d.step(e.memset(mask4[:, :, 0:1], -BIG))
                d.step(e.tensor_copy(iota_b[:, :], con("iota")))
                d.step(e.memset(count[:, :], 0.0))
            d.settle()
            if n:
                e.wait_ge(rows_done, (EPIECE if n == 1 else EPIECE + TPIECE) + OPEN)
                d.step(e.tensor_copy(ends[:, n - 1, 0:20].rearrange("p (q o) -> p q o", o=1),
                                     sums[:, :, :, U:U + 1].rearrange("p q h o -> p (q h) o")))
                d.step(e.tensor_copy(ends[:, n - 1, 20:24].rearrange("p (q o) -> p q o", o=1),
                                     run_max[:, :, U:U + 1]))
                d.settle()
            if n < 2:
                d.step(e.tensor_copy(adst[:, :, U:U + 1], first[n][:, GC + GH:ROW].unsqueeze(2)))
                d.step(e.memset(run_max[:, :, U:U + 1], -BIG))
                d.step(e.memset(sums[:, :, :, U:U + 1], 0.0))

        DVE_C = 23

        def chunk_dve(e, c, par, i, at, experts):
            base = c * DVE_C
            col, pad = at
            step = [0]

            def own(ins):
                step[0] += 1
                ins.then_inc(chunk_step, 1)

            def settle():
                e.wait_ge(chunk_step, base + step[0] + OPEN)

            k = keys[marks["sorted"][1]][:, bass.ds(col, U)].bitcast(I32)
            own(e.tensor_scalar(hilo_i[:, 0], k, SRC_BITS + 7, None, ALU.logical_shift_right))
            own(e.tensor_scalar(hilo_i[:, 1], k, SRC_BITS, P - 1, ALU.logical_shift_right, ALU.bitwise_and))
            settle()
            own(e.tensor_scalar(hilo[:, 0], hilo_i[:, 0], -float(KEY_BASE // P), None, ALU.add))
            own(e.tensor_copy(hilo[:, 1], hilo_i[:, 1]))
            settle()
            for q in range(U // 8):
                e.wait_ge(counted, c * 8 + q - 1 + OPEN)
                hb = hot_b[q % 2]
                for j in range(8):
                    jj = 8 * q + j
                    e.tensor_scalar(hb[:, j, 0:P], iota_b[:, 0:P], hilo[:, 1, jj:jj + 1], None, ALU.is_equal)
                    h = e.tensor_scalar(hb[:, j, P:384], iota_b[:, :], hilo[:, 0, jj:jj + 1], None, ALU.is_equal)
                h.then_inc(hot_ready, 1)
            if experts:
                for t in range(4):
                    b = t % 2
                    e.wait_ge(y_full[b], c * 2 + t // 2 + 1 + OPEN)
                    e.wait_ge(y_saved, c - 1 + OPEN)
                    e.tensor_tensor(yt[par][:, t, :], bank[:, 2 + b, :],
                                    b2_s[:, :, :].rearrange("p e c -> p (e c)"), ALU.add).then_inc(y_evac[b], 1)
            now = dst_f[:, bass.ds(col + pad + 1, U)].unsqueeze(1).broadcast_to([P, GH, U])
            before = dst_f[:, bass.ds(col + pad, U)].unsqueeze(1).broadcast_to([P, GH, U])
            own(e.tensor_tensor(new4[:, :, :], now, before, ALU.not_equal))
            own(e.tensor_tensor(keep4[:, :, 1:], now, before, ALU.is_equal))
            settle()
            own(e.tensor_scalar(mask4[:, :, 1:], keep4[:, :, 1:], -1.0, BIG, ALU.add, ALU.mult))
            own(e.tensor_copy(adst_in[:, :, 0:1], adst[:, :, U:U + 1]))
            e.wait_ge(gathered[par], (i + 1) * (16 * U))
            g = gath[par][:, :, :].rearrange("p j r -> p r j")
            own(e.tensor_tensor(adst_in[:, :, 1:], new4[:, :, :], g[:, GC + GH:ROW], ALU.mult))
            settle()
            own(e.tensor_tensor_scan(flat(adst), flat(keep4), flat(adst_in), 0.0, ALU.mult, ALU.add))
            settle()
            own(e.tensor_tensor(logit[:, :, 1:], adst[:, :, 1:], g[:, GC:GC + GH], ALU.add))
            settle()
            own(e.scalar_tensor_tensor(leaky[:, :, 1:], logit[:, :, 1:], 0.2, logit[:, :, 1:], ALU.mult, ALU.max))
            own(e.tensor_copy(leaky[:, :, 0:1], run_max[:, :, U:U + 1]))
            e.wait_ge(rows_done, c + OPEN)
            settle()
            own(e.tensor_tensor_scan(flat(run_max), flat(mask4), flat(leaky), 0.0, ALU.add, ALU.max))
            settle()
            own(e.tensor_tensor(diff[:, 0, :, 1:], run_max[:, :, 0:U], mask4[:, :, 1:], ALU.add))
            own(e.tensor_tensor(diff[:, 1, :, 1:], leaky[:, :, 1:], run_max[:, :, 1:], ALU.subtract))
            settle()
            e.tensor_tensor(diff[:, 0, :, 1:], diff[:, 0, :, 1:], run_max[:, :, 1:],
                            ALU.subtract).then_inc(diff_ready, 1)
            own(e.tensor_copy(weight[:, 1, :, 0:1], sums[:, 0, :, U:U + 1]))
            own(e.tensor_copy(terms[:, :, :, 0:1], sums[:, 1:, :, U:U + 1]))
            e.wait_ge(weights_ready, c + 1 + OPEN)
            e.tensor_tensor(terms[:, :, :, 1:], weight[:, 1:2, :, 1:].broadcast_to([P, NE, GH, U]),
                            g[:, 0:GC].rearrange("p (h e) j -> p e h j", e=NE), ALU.mult).then_inc(edge_used, 1)
            e.wait_ge(edge_used, c + 1 + OPEN)
            settle()
            for q in range(1 + NE):
                data = flat3(weight[:, 1]) if q == 0 else flat3(terms[:, q - 1])
                own(e.tensor_tensor_scan(flat3(sums[:, q]), flat3(weight[:, 0]), data, 0.0, ALU.mult, ALU.add))
            settle()
            assert step[0] == DVE_C, step[0]
            e.wait_ge(counted, c * 8 + 8 + OPEN)
            e.wait_ge(count_added, c + OPEN)
            e.tensor_tensor(count[:, :], count[:, :], bank[:, 4 + par, 0:256], ALU.add).then_inc(count_added, 1)

        def flat(t):
            return t[:, :, :].rearrange("p h j -> p (h j)")

        def flat3(a):
            return a.rearrange("p h j -> p (h j)")

        def chunk_pe(e, c, par, i, experts):
            for q in range(U // 8):
                e.wait_ge(hot_ready, c * 8 + q + 1 + OPEN)
                if q == 0:
                    e.wait_ge(count_added, c - 1 + OPEN)
                hb = hot_b[q % 2]
                for j in range(8):
                    m = e.matmul(bank[:, 4 + par, 0:256], hb[:, j, 0:P], hb[:, j, P:384],
                                 start=q == 0 and j == 0, stop=q == U // 8 - 1 and j == 7)
                m.then_inc(counted, 1)
            if not experts:
                return
            e.wait_ge(xm_loaded[par], (i + 1) * 16)
            for k in range(2 * NE):
                e.wait_ge(hidden, c * 8 + k - 1 + OPEN)
                e.matmul(bank[:, k % 2, :], w1_s[:, k // 2, P * (k % 2):P * (k % 2) + P], xm[par][:, :],
                         start=True, stop=True).then_inc(up_full, 1)
            e.wait_ge(hidden, c * 8 + 8 + OPEN)
            for t in range(4):
                b = t % 2
                e.wait_ge(y_evac[b], c * 2 + t // 2 + OPEN)
                for k in range(2 * NE):
                    m = e.matmul(bank[:, 2 + b, C * (k // 2):C * (k // 2) + C], hid[:, k, P * t:P * t + P],
                                 w2_s[:, k // 2, k % 2, :], start=k % 2 == 0, stop=k % 2 == 1)
                m.then_inc(y_full[b], 1)

        def chunk_act(e, c, par, i, experts):
            if experts:
                e.wait_ge(y_full[1], c * 2 + OPEN)
                for k in range(2 * NE):
                    e.wait_ge(up_full, c * 8 + k + 1 + OPEN)
                    e.activation(hid[:, k, :], bank[:, k % 2, :], ACT.Gelu,
                                 bias=b1_s[:, k // 2, k % 2:k % 2 + 1]).then_inc(hidden, 1)
            e.wait_ge(diff_ready, c + 1 + OPEN)
            e.activation(weight[:, :, :, 1:].rearrange("p a h j -> p (a h) j"),
                         diff[:, :, :, 1:].rearrange("p a h j -> p (a h) j"), ACT.Exp).then_inc(weights_ready, 1)
            e.wait_ge(chunk_step, c * DVE_C + DVE_C + OPEN)
            e.wait_ge(rows_saved, c - 1 + OPEN)
            rw = rows[par][:, :, :].rearrange("p j r -> p r j")
            e.activation(rw[:, 0:20], sums[:, :, :, 1:].rearrange("p q h j -> p (q h) j"), ACT.Copy)
            e.activation(rw[:, 20:24], run_max[:, :, 1:], ACT.Copy).then_inc(rows_done, 1)

        def chunk_pool(e, c, par, i, col):
            e.wait_ge(edge_used, c - 1 + OPEN)
            e.tensor_copy(idx[par][:, :], keys[1 - marks["sorted"][1]][:, bass.ds(col, U)].bitcast(I32)).then_inc(idx_ready, 1)
            e.wait_ge(idx_ready, c + 1 + OPEN)
            e.sem_inc(idx_taken, 1)
            for j in range(U):
                e.indirect_dma_start(gath[par][:, j, :], None, node_rows,
                                     bass.IndirectOffsetOnAxis(ap=idx[par][:, j:j + 1].bitcast(U32), axis=0)
                                     ).then_inc(gathered[par], 16)

        def last_dst(n):
            return dst_f[:, EC:EC + 1] if n == 0 else dst_f[:, EC + TC + 1:]

        def first_dst(n):
            return dst_f[:, 1:2] if n == 0 else dst_f[:, EC + 2:EC + 3]

        def dve_run_rows(d):
            e = d.eng
            for n, (a, w) in enumerate(((1, EC), (EC + 2, TC))):
                d.step(e.tensor_scalar(run_flag[:, 0:w], dst_f[:, a:a + w], first_dst(n), None, ALU.is_equal))
                d.settle()
                d.step(e.tensor_reduce(run_len[:, n:n + 1], run_flag[:, 0:w], AX, ALU.add))
                d.settle()
            d.step(e.tensor_tensor(row_i[:, :], run_len[:, :], con("row_base"), ALU.add))

        def dve_join(d):
            e = d.eng
            e.wait_ge(prefix_full, 1)
            d.step(e.tensor_copy(tot[:, 0], bank[:, 7, 0:256]))
            d.settle()
            d.step(e.tensor_tensor_scan(tot[:, 1], tot[:, 0], tot[:, 0], 0.0, ALU.add, ALU.max))
            d.step(e.tensor_scalar(end_f[:, :], bank[:, 6, 0:256], -1.0, None, ALU.add))
            d.settle()
            d.step(e.tensor_tensor(end_f[:, :], end_f[:, :], tot[:, 1], ALU.add))
            d.settle()
            d.step(e.tensor_tensor(end_i[:, :], end_f[:, :], tot[:, 0], ALU.subtract))
            for n in range(2):
                d.step(e.tensor_copy(chain_in[:, n, 0].rearrange("p (q h) -> p q h", h=GH),
                                     ends[:, n, 20:24].unsqueeze(1).broadcast_to([P, 5, GH])))
                d.step(e.tensor_copy(chain_in[:, n, 1], ends[:, n, 0:20]))
                d.step(e.tensor_copy(chain_in[:, n, 2], last_dst(n).broadcast_to([P, 20])))
                d.step(e.tensor_copy(chain_in[:, n, 3], first_dst(n).broadcast_to([P, 20])))
            d.step(e.memset(chain[:, :, 0:1], -1.0))
            d.step(e.memset(ck[:, 0, 0:1], 0.0))
            d.step(e.memset(ck[:, 2, 0:1], -BIG))
            d.settle()
            e.sem_inc(chain_ready, 1)
            e.wait_ge(chain_turned, 1)
            d.step(e.tensor_copy(chain[:, :, 1:].rearrange("q k (n p) -> q n k p", n=2),
                                 bank[0:20, 0:2, :].rearrange("q n (k p) -> q n k p", k=4)))
            d.settle()
            big, den, last, frst = (chain[:, k, 1:] for k in range(4))
            prev_last = chain[:, 2, 0:256]
            keep, mask, diffs = ck[:, 1, 1:], ck[:, 5, 1:], ck[:, 3:5, 1:]
            d.step(e.tensor_tensor(keep, last, prev_last, ALU.is_equal))
            d.settle()
            d.step(e.tensor_scalar(mask, keep, -1.0, BIG, ALU.add, ALU.mult))
            d.settle()
            d.step(e.tensor_tensor_scan(ck[:, 2, 1:], mask, big, -BIG, ALU.add, ALU.max))
            d.settle()
            d.step(e.tensor_tensor(ck[:, 3, 1:], ck[:, 2, 0:256], mask, ALU.add))
            d.step(e.tensor_tensor(ck[:, 4, 1:], big, ck[:, 2, 1:], ALU.subtract))
            d.settle()
            d.step(e.tensor_tensor(ck[:, 3, 1:], ck[:, 3, 1:], ck[:, 2, 1:], ALU.subtract))
            d.settle()
            e.sem_inc(chain_diff, 1)
            e.wait_ge(chain_exp, 1)
            d.step(e.tensor_tensor(ck[:, 4, 1:], ck[:, 4, 1:], den, ALU.mult))
            d.step(e.tensor_tensor(ck[:, 5, 1:], frst, prev_last, ALU.is_equal))
            d.settle()
            d.step(e.tensor_tensor_scan(ck[:, 0, 1:], ck[:, 3, 1:], ck[:, 4, 1:], 0.0, ALU.mult, ALU.add))
            d.step(e.tensor_scalar(ck[:, 5, 1:], ck[:, 5, 1:], -1.0, BIG, ALU.add, ALU.mult))
            d.settle()
            d.step(e.tensor_tensor(joined[:, 0], ck[:, 2, 0:256], ck[:, 5, 1:], ALU.add))
            d.step(e.tensor_copy(joined[:, 1], ck[:, 0, 0:256]))
            d.settle()
            e.sem_inc(chain_ready, 1)
            e.wait_ge(chain_turned, 2)
            d.step(e.tensor_copy(carry[:, :, :, :].rearrange("p n k q -> p (n k q)"), bank[:, 2, 0:80]))
            e.wait_ge(run_got, 32)
            d.settle()
            rmax, rin = at_run[:, :, 20:24], carry[:, :, 0, 0:4]
            new, own_d, in_d = (jw[:, k] for k in range(3))
            d.step(e.tensor_tensor(new, rmax, rin, ALU.max))
            d.settle()
            d.step(e.tensor_tensor(own_d, rmax, new, ALU.subtract))
            d.step(e.tensor_tensor(in_d, rin, new, ALU.subtract))
            d.settle()
            e.sem_inc(chain_diff, 1)
            e.wait_ge(chain_exp, 2)
            sm = at_run[:, :, 0:20].rearrange("p n (q h) -> p n q h", h=GH)
            ci = carry[:, :, 1, :].rearrange("p n (q h) -> p n q h", h=GH)
            d.step(e.tensor_tensor(sm, sm, own_d.unsqueeze(2).broadcast_to([P, 2, 5, GH]), ALU.mult))
            d.step(e.tensor_tensor(ci, ci, in_d.unsqueeze(2).broadcast_to([P, 2, 5, GH]), ALU.mult))
            d.settle()
            d.step(e.tensor_tensor(sm, sm, ci, ALU.add))
            d.step(e.tensor_copy(rmax, new))
            d.settle()
            e.sem_inc(runs_joined, 1)

        def pe_join(e):
            e.wait_ge(count_added, EPIECE + TPIECE + OPEN)
            e.matmul(bank[:, 6, 0:256], con("upper"), count[:, :], start=True, stop=True)
            e.matmul(bank[:, 7, 0:256], con("ones"), count[:, :], start=True, stop=True).then_inc(prefix_full, 1)
            e.wait_ge(chain_ready, 1)
            for n in range(2):
                for k in range(4):
                    t = e.transpose(bank[0:20, n, P * k:P * k + P], chain_in[:, n, k, :], con("ident"))
            t.then_inc(chain_turned, 1)
            e.wait_ge(chain_ready, 2)
            for n in range(2):
                for k in range(2):
                    t = e.transpose(bank[:, 2, 20 * (2 * n + k):20 * (2 * n + k) + 20],
                                    joined[:, k, P * n:P * n + P], con("ident")[0:20, 0:20])
            t.then_inc(chain_turned, 1)

        def act_join(e):
            e.wait_ge(chain_diff, 1)
            e.activation(ck[:, 3:5, 1:], ck[:, 3:5, 1:], ACT.Exp).then_inc(chain_exp, 1)
            e.wait_ge(chain_diff, 2)
            e.activation(jw[:, 1:3], jw[:, 1:3], ACT.Exp).then_inc(chain_exp, 1)

        def pool_join(e):
            e.wait_ge(rows_saved, EPIECE + TPIECE + OPEN)
            for n in range(2):
                e.indirect_dma_start(at_run[:, n, :], None, edge_rows,
                                     bass.IndirectOffsetOnAxis(ap=row_i[:, n:n + 1].bitcast(U32), axis=0)
                                     ).then_inc(run_got, 16)
            e.wait_ge(run_got, 32)
            e.wait_ge(runs_joined, 1)
            for n in range(2):
                e.indirect_dma_start(edge_rows, bass.IndirectOffsetOnAxis(ap=row_i[:, n:n + 1].bitcast(U32), axis=0),
                                     at_run[:, n, :], None).then_inc(run_put, 16)
            e.wait_ge(run_put, 32)

        DVE_D = 24 + 8 * 12

        def group_dve(e, g, par, i):
            base = g * DVE_D
            n_own = [0]

            def own(ins):
                n_own[0] += 1
                ins.then_inc(gate_step, 1)

            def settle():
                e.wait_ge(gate_step, base + n_own[0] + OPEN)

            def each(v, shape):
                return v.unsqueeze(len(v.shape)).broadcast_to(shape)

            r = got[par][:, :, :]
            wide, nar = [P, 32, GC], [P, 32, NE]
            e.wait_ge(got_landed[par], (i + 1) * (16 * 32))
            own(e.tensor_scalar(s4[:, 0], r[:, :, 0:GH], DEN_EPS, None, ALU.add))
            settle()
            own(e.reciprocal(s4[:, 1], s4[:, 0]))
            settle()
            own(e.tensor_tensor(sc[:, 0].rearrange("p n (h e) -> p n h e", e=NE),
                                r[:, :, GH:20].rearrange("p n (e h) -> p n h e", h=GH),
                                each(s4[:, 1], [P, 32, GH, NE]), ALU.mult))
            settle()
            own(e.tensor_tensor(sc[:, 0], sc[:, 0], gate_s[:, 0:GC].unsqueeze(1).broadcast_to(wide), ALU.add))
            settle()
            own(e.tensor_reduce(s1[:, 0], sc[:, 0], AX, ALU.add))
            settle()
            own(e.tensor_scalar(s1[:, 1], s1[:, 0], 1.0 / GC, None, ALU.mult))
            settle()
            own(e.tensor_tensor(sc[:, 1], sc[:, 0], each(s1[:, 1], wide), ALU.subtract))
            settle()
            own(e.tensor_tensor(sc[:, 2], sc[:, 1], sc[:, 1], ALU.mult))
            settle()
            own(e.tensor_reduce(s1[:, 2], sc[:, 2], AX, ALU.add))
            settle()
            e.sem_inc(gate_asks, 1)
            e.wait_ge(gate_std, g + 1 + OPEN)
            own(e.reciprocal(s1[:, 4], s1[:, 3]))
            settle()
            own(e.tensor_tensor(sc[:, 2], sc[:, 1], each(s1[:, 4], wide), ALU.mult))
            settle()
            own(e.tensor_tensor(sc[:, 1], sc[:, 2], gate_s[:, GC:2 * GC].unsqueeze(1).broadcast_to(wide), ALU.mult))
            settle()
            own(e.tensor_tensor(sc[:, 2], sc[:, 1], gate_s[:, 2 * GC:].unsqueeze(1).broadcast_to(wide), ALU.add))
            settle()
            own(e.tensor_reduce(s4[:, 2], sc[:, 2].rearrange("p n (h e) -> p n e h", e=NE), AX, ALU.add))
            settle()
            mine = each(s4[:, 2], [P, 32, NE, NE])
            other = s4[:, 2].unsqueeze(2).broadcast_to([P, 32, NE, NE])
            gt, eq = (sc[:, k].rearrange("p n (e f) -> p n e f", f=NE) for k in (0, 1))
            own(e.tensor_tensor(gt, other, mine, ALU.is_gt))
            own(e.tensor_tensor(eq, other, mine, ALU.is_equal))
            own(e.tensor_reduce(s1[:, 5], s4[:, 2], AX, ALU.max))
            settle()
            own(e.tensor_tensor(sc[:, 2], sc[:, 1], con("earlier").unsqueeze(1).broadcast_to(wide), ALU.mult))
            own(e.tensor_tensor(s4[:, 3], s4[:, 2], each(s1[:, 5], nar), ALU.subtract))
            settle()
            e.sem_inc(gate_asks2, 1)
            own(e.tensor_tensor(sc[:, 1], sc[:, 0], sc[:, 2], ALU.add))
            settle()
            own(e.tensor_reduce(s4[:, 4], sc[:, 1].rearrange("p n (e f) -> p n e f", f=NE), AX, ALU.add))
            settle()
            e.wait_ge(gate_exp, g + 1 + OPEN)
            own(e.scalar_tensor_tensor(s4[:, 5], s4[:, 4], 1.5, s4[:, 3], ALU.is_lt, ALU.mult))
            settle()
            own(e.tensor_reduce(s1[:, 6], s4[:, 5], AX, ALU.add))
            settle()
            own(e.reciprocal(s1[:, 7], s1[:, 6]))
            settle()
            e.tensor_tensor(gates[par][:, :, :], s4[:, 5], each(s1[:, 7], nar), ALU.mult).then_inc(gates_ready, 1)
            e.wait_ge(gates_ready, g + 1 + OPEN)
            for k in range(8):
                b = k % 2
                yv = yo[b][:, :, :].rearrange("p h (e c) -> p h e c", e=NE)
                e.wait_ge(yo_loaded[b], g * 64 + 16 * (k // 2 + 1))
                e.wait_ge(mix_turned, g * 8 + k - 1 + OPEN)
                for ex in range(NE):
                    for h in range(4):
                        gate = gates[par][:, 4 * k + h, ex:ex + 1]
                        if ex == 0:
                            own(e.tensor_scalar(mix[b][:, h], yv[:, h, ex], gate, None, ALU.mult))
                        elif ex < NE - 1:
                            own(e.scalar_tensor_tensor(mix[b][:, h], yv[:, h, ex], gate, mix[b][:, h], ALU.mult,
                                                       ALU.add))
                        else:
                            m = e.scalar_tensor_tensor(mix[b][:, h], yv[:, h, ex], gate, mix[b][:, h], ALU.mult,
                                                       ALU.add)
                    settle()
                m.then_inc(mix_ready, 1)
                e.wait_ge(mix_turned, g * 8 + k + 1 + OPEN)
                e.wait_ge(res_loaded[b], g * 64 + 16 * (k // 2 + 1))
                e.wait_ge(fin_saved, g * 8 + k - 1 + OPEN)
                e.tensor_tensor(fin[b][:, :], bank[:, 2 + b, :], res[b][:, :], ALU.add).then_inc(fin_ready, 1)
            assert n_own[0] == DVE_D, n_own[0]

        def group_pe(e, g):
            for k in range(8):
                e.wait_ge(mix_ready, g * 8 + k + 1 + OPEN)
                e.wait_ge(fin_ready, g * 8 + k - 1 + OPEN)
                for h in range(4):
                    t = e.transpose(bank[:, 2 + k % 2, P * h:P * h + P], mix[k % 2][:, h, :], con("ident"))
                t.then_inc(mix_turned, 1)

        def group_act(e, g):
            e.wait_ge(gate_asks, g + 1 + OPEN)
            e.activation(s1[:, 3], s1[:, 2], ACT.Sqrt, bias=eps[:, 1:2], scale=1.0 / GC).then_inc(gate_std, 1)
            e.wait_ge(gate_asks2, g + 1 + OPEN)
            e.activation(s4[:, 3], s4[:, 3], ACT.Exp, scale=1.0 / GH).then_inc(gate_exp, 1)

        def group_pool(e, g, par, i):
            e.wait_ge(gates_ready, g - 1 + OPEN)
            e.tensor_copy(idx_d[par][:, :], end_i[:, bass.ds(g * 32, 32)]).then_inc(idx_d_ready, 1)
            e.wait_ge(idx_d_ready, g + 1 + OPEN)
            e.sem_inc(idx_taken, 1)
            for j in range(32):
                e.indirect_dma_start(got[par][:, j, :], None, edge_rows,
                                     bass.IndirectOffsetOnAxis(ap=idx_d[par][:, j:j + 1].bitcast(U32), axis=0)
                                     ).then_inc(got_landed[par], 16)

        @block.vector
        def _(e):
            for t in (biased, max_ready, inv_ready, rstd_ready, dve_own, chunk_step, hot_ready, diff_ready,
                      edge_used, count_added, *y_evac, gate_step, gates_ready, mix_ready, fin_ready,
                      gate_asks, gate_asks2):
                e.sem_inc(t, OPEN)
            d = Done(e, key_step)
            dve_setup(d)
            dve_sort(d)
            with e.Fori(0, STRIPS // 2) as i:
                for par in range(2):
                    strip_dve(e, i * 2 + par, par, 0 if par == 0 else (i % 8) // 7)
            j = Done(e, join_step)
            e.wait_ge(strip_saved, STRIPS + OPEN)
            dve_run_rows(j)
            piece_start(j, 0)
            with e.Fori(0, EPIECE // 2) as i:
                for par in range(2):
                    chunk_dve(e, i * 2 + par, par, i, ((i * 2 + par) * U, 0), True)
            piece_start(j, 1)
            with e.Fori(EPIECE // 2, (EPIECE + TPIECE) // 2) as i:
                for par in range(2):
                    chunk_dve(e, i * 2 + par, par, i, ((i * 2 + par) * U, 1), False)
            piece_start(j, 2)
            dve_join(j)
            with e.Fori(0, 4) as i:
                for par in range(2):
                    group_dve(e, i * 2 + par, par, i)

        @block.tensor
        def _(e):
            for t in (*full, s_full, *pt_full, counted, up_full, *y_full, mix_turned):
                e.sem_inc(t, OPEN)
            pe_setup(e)
            pe_sort(e)
            with e.Fori(0, STRIPS // 2) as i:
                for par in range(2):
                    strip_pe(e, i * 2 + par, par, i)
            e.wait_ge(experts_loaded, 16 * 5)
            with e.Fori(0, EPIECE // 2) as i:
                for par in range(2):
                    chunk_pe(e, i * 2 + par, par, i, True)
            with e.Fori(EPIECE // 2, (EPIECE + TPIECE) // 2) as i:
                for par in range(2):
                    chunk_pe(e, i * 2 + par, par, i, False)
            pe_join(e)
            with e.Fori(0, 4) as i:
                for par in range(2):
                    group_pe(e, i * 2 + par)

        @block.scalar
        def _(e):
            for t in (*evac, exp_ready, *pt_evac, hidden, weights_ready, rows_done, gate_std, gate_exp):
                e.sem_inc(t, OPEN)
            act_sort(e)
            with e.Fori(0, STRIPS // 2) as i:
                for par in range(2):
                    strip_act(e, i * 2 + par, par)
            e.wait_ge(strip_saved, STRIPS + OPEN)
            e.wait_ge(experts_loaded, 16 * 5)
            with e.Fori(0, EPIECE // 2) as i:
                for par in range(2):
                    chunk_act(e, i * 2 + par, par, i, True)
            with e.Fori(EPIECE // 2, (EPIECE + TPIECE) // 2) as i:
                for par in range(2):
                    chunk_act(e, i * 2 + par, par, i, False)
            act_join(e)
            with e.Fori(0, 4) as i:
                for par in range(2):
                    group_act(e, i * 2 + par)

        @block.gpsimd
        def _(e):
            for t in (xn_done, centered, probs_ready, idx_ready, idx_d_ready):
                e.sem_inc(t, OPEN)
            e.iota(loops_i[:, 0], [[-P, 32], [-EC, 8]], base=M - 1 + (KEY_BASE), channel_multiplier=-1
                   ).then_inc(self_loops, 1)
            e.wait_ge(vec_sums, 2)
            e.memset(vb[:, :, :, :, :], 0.0).then_inc(vb_zero, 1)
            with e.Fori(0, STRIPS // 2) as i:
                for par in range(2):
                    strip_pool(e, i * 2 + par, par)
            e.wait_ge(strip_saved, STRIPS + OPEN)
            e.wait_ge(sorted_, 1)
            for n in range(2):
                e.indirect_dma_start(first[n][:, :], None, node_rows, bass.IndirectOffsetOnAxis(
                    ap=first_row_i[:, n:n + 1].bitcast(U32), axis=0)).then_inc(first_got, 16)
            with e.Fori(0, (EPIECE + TPIECE) // 2) as i:
                for par in range(2):
                    chunk_pool(e, i * 2 + par, par, i, (i * 2 + par) * U)
            pool_join(e)
            with e.Fori(0, 4) as i:
                for par in range(2):
                    group_pool(e, i * 2 + par, par, i)

        @block.sync
        def _(e):
            for t in (strip_saved, y_saved, rows_saved, fin_saved):
                e.sem_inc(t, OPEN)
            rest = REL - P
            loads = (
                (cst[:, :], const),
                (edge_i[:, 0, :], edges[0].rearrange("(p f) -> p f", p=P)),
                (edge_i[:, 1, :], edges[1].rearrange("(p f) -> p f", p=P)),
                (hot[:, 0, :], rel_hot[0:P, :]), (hot[0:rest, 1, :], rel_hot[P:REL, :]),
                (table_s[:, 0, :], bias_table[0:P, :]), (table_s[0:rest, 1, :], bias_table[P:REL, :]),
                (wq_s[:, :], wq_t), (wkv_s[:, :], wkv_t), (wproj_s[:, :], wproj_t),
                (vec[:, 0:1], bq.unsqueeze(1)), (vec[:, 1:2], bkv[0:C].unsqueeze(1)),
                (vec[:, 2:3], bkv[C:2 * C].unsqueeze(1)), (vec[:, 3:4], bproj.unsqueeze(1)),
                (wgat_s[:, :], w_gat),
                (att_s[:, 0:GC], att_src.rearrange("a b -> (a b)").partition_broadcast(P)),
                (att_s[:, GC:2 * GC], att_dst.rearrange("a b -> (a b)").partition_broadcast(P)),
                (gate_s[:, 0:GC], b_gat.partition_broadcast(P)),
                (gate_s[:, GC:2 * GC], ln_gamma.partition_broadcast(P)),
                (gate_s[:, 2 * GC:3 * GC], ln_beta.partition_broadcast(P)),
            )
            assert len(loads) == N_LOADS
            for dst, src in loads:
                e.dma_start(dst, src).then_inc(loaded, 16)
            xv = x.rearrange("b c h w -> c b (h w)")
            ov = out.rearrange("b c h w -> c b (h w)")
            nodes = node_rows.rearrange("(n p) r -> p n r", p=P)

            def row_of(s, j):
                r = s % 16
                return s // 16, (r * WS + SS if j == 0 else ((r + 1) % 16) * WS)

            def load_strip(s, par):
                for j in range(2):
                    img, row = row_of(s, j)
                    src = xv[:, bass.ds(img, 1), bass.ds(row * W, HTOK)] if not isinstance(s, int) else \
                        xv[:, img:img + 1, row * W:row * W + HTOK]
                    e.dma_start(xt[par][:, 4 * j:4 * j + 4, :].rearrange("c i w -> c (i w)"),
                                src.rearrange("c b t -> c (b t)")).then_inc(x_loaded[par], 16)

            def store_strip(s, par, i):
                wait_evac(e, s, 15)
                e.wait_ge(xn_done, s * 4 + 4 + OPEN)
                e.wait_ge(dve_own, s * 6 + 6 + OPEN)
                for j in range(2):
                    img, row = row_of(s, j)
                    n = img * H + row
                    rws = slice(4 * j, 4 * j + 4)
                    at = bass.ds(n * W, HTOK)
                    e.dma_start(x1_dram[:, at], x1[par][:, rws, :].rearrange("c i w -> c (i w)")
                                ).then_inc(strip_stored[par], 16)
                    e.dma_start(xn_dram[:, at], x2[par][:, rws, :].rearrange("c i w -> c (i w)")
                                ).then_inc(strip_stored[par], 16)
                    e.dma_start(nodes[:, bass.ds(n, 4), :], node[par][:, rws, :]).then_inc(strip_stored[par], 16)
                e.wait_ge(strip_stored[par], (i + 1) * 96)
                e.sem_inc(strip_saved, 1)

            e.wait_ge(vec_sums, 2)
            load_strip(0, 0)
            load_strip(1, 1)
            with e.Fori(0, STRIPS // 2 - 1) as i:
                for par in range(2):
                    store_strip(i * 2 + par, par, i)
                    load_strip(i * 2 + par + 2, par)
            for par in range(2):
                store_strip(STRIPS - 2 + par, par, STRIPS // 2 - 1)

            for dst, src in ((w1_s[:, :, :], w1.rearrange("e c f -> c e f")),
                             (w2_s[:, :, 0, :], w2[:, 0:P, :].rearrange("e f c -> f e c")),
                             (w2_s[:, :, 1, :], w2[:, P:FF, :].rearrange("e f c -> f e c")),
                             (b1_s[:, :, :].rearrange("p e k -> p (e k)"), b1),
                             (b2_s[:, :, :].rearrange("p e c -> p (e c)"),
                              b2.rearrange("e c -> (e c)").partition_broadcast(P))):
                e.dma_start(dst, src).then_inc(experts_loaded, 16)

            main = edge_rows[0:EDGES, :].rearrange("(p f) r -> p f r", p=P)
            tail = edge_rows[EDGES:MERGED, :].rearrange("(p f) r -> p f r", p=P)

            def load_tokens(c, par):
                e.dma_start(xm[par][:, :], xn_dram[:, bass.ds(c * 512, 512)]).then_inc(xm_loaded[par], 16)

            def chunk_sp(c, par, i, piece, col, experts, more):
                if more:
                    e.wait_ge(up_full, c * 8 + 8 + OPEN)
                    load_tokens(c + 2, par)
                if experts:
                    e.wait_ge(y_evac[0], c * 2 + 2 + OPEN)
                    e.wait_ge(y_evac[1], c * 2 + 2 + OPEN)
                    e.dma_start(y_dram[bass.ds(c * 4, 4)].rearrange("h p f -> p h f"), yt[par][:, :, :]
                                ).then_inc(y_stored, 16)
                e.wait_ge(rows_done, c + 1 + OPEN)
                e.dma_start(piece[:, bass.ds(col, U), :], rows[par][:, :, :]).then_inc(rows_stored, 16)
                if experts:
                    e.wait_ge(y_stored, (c + 1) * 16)
                    e.sem_inc(y_saved, 1)
                e.wait_ge(rows_stored, (c + 1) * 16)
                e.sem_inc(rows_saved, 1)

            load_tokens(0, 0)
            load_tokens(1, 1)
            with e.Fori(0, EPIECE // 2 - 1) as i:
                for par in range(2):
                    chunk_sp(i * 2 + par, par, i, main, (i * 2 + par) * U, True, True)
            for par in range(2):
                c = EPIECE - 2 + par
                chunk_sp(c, par, c // 2, main, c * U, True, False)
            with e.Fori(EPIECE // 2, (EPIECE + TPIECE) // 2) as i:
                for par in range(2):
                    chunk_sp(i * 2 + par, par, i, tail, (i * 2 + par - EPIECE) * U, False, False)

            def load_quad(t, b):
                e.dma_start(yo[b][:, :, :], y_dram[bass.ds(t * 4, 4)].rearrange("h p f -> p h f")
                            ).then_inc(yo_loaded[b], 16)
                e.dma_start(res[b][:, :], x1_dram[:, bass.ds(t * 512, 512)]).then_inc(res_loaded[b], 16)

            def store_quad(t, k, n):
                b = k % 2
                e.wait_ge(fin_ready, n + 1 + OPEN)
                e.dma_start(ov[:, bass.ds(t // 32, 1), bass.ds((t % 32) * 512, 512)].rearrange("c b t -> c (b t)"),
                            fin[b][:, :]).then_inc(out_stored[b], 16)

            e.wait_ge(runs_joined, 1)
            e.wait_ge(run_put, 32)
            load_quad(0, 0)
            load_quad(1, 1)
            with e.Fori(0, 31) as q:
                for b in range(2):
                    store_quad(q * 2 + b, b, q * 2 + b)
                    load_quad(q * 2 + b + 2, b)
                    e.wait_ge(out_stored[b], (q + 1) * 16)
                    e.sem_inc(fin_saved, 1)
            for b in range(2):
                store_quad(62 + b, b, 62 + b)
                e.wait_ge(out_stored[b], 32 * 16)


def kernel(**inputs):
    import concourse.bacc as bacc
    from concourse.bass_utils import run_bass_kernel_spmd

    nc = bacc.Bacc("TRN2", target_bir_lowering=False, num_devices=1)
    laid = {
        "x": inputs["x"],
        "wq_t": np.asarray(inputs["L0_conv_Wq"]).T,
        "bq": inputs["L0_conv_bq"],
        "wkv_t": np.asarray(inputs["L0_conv_Wkv"]).T,
        "bkv": inputs["L0_conv_bkv"],
        "wproj_t": np.asarray(inputs["L0_conv_Wproj"]).T,
        "bproj": inputs["L0_conv_bproj"],
        "bias_table": inputs["L0_conv_bias_table"],
        "w_gat": inputs["L0_ffn_W_gat"],
        "att_src": inputs["L0_ffn_att_src"],
        "att_dst": inputs["L0_ffn_att_dst"],
        "b_gat": inputs["L0_ffn_b_gat"],
        "ln_gamma": inputs["L0_ffn_ln_gamma"],
        "ln_beta": inputs["L0_ffn_ln_beta"],
        "w1": inputs["L0_ffn_W1"],
        "b1": np.asarray(inputs["L0_ffn_b1"]).reshape(NE * 2, P).T,
        "w2": inputs["L0_ffn_W2"],
        "b2": inputs["L0_ffn_b2"],
        "edges": inputs["L0_ffn_edge_index"],
        "const": constants(),
        "rel_hot": relative_one_hot(),
    }
    arrays, args = {}, []
    for name, value in laid.items():
        a = np.ascontiguousarray(value)
        arrays[f"in_{name}"] = a
        args.append(nc.dram_tensor(f"in_{name}", a.shape, mybir.dt.from_np(a.dtype), kind="ExternalInput").ap())
    args.append(nc.dram_tensor("out", (IMGS, C, H, W), F32, kind="ExternalOutput").ap())
    program(nc, *args)
    r = run_bass_kernel_spmd(nc, [arrays], core_ids=[0])
    return r.results[0]["out"]
```

```python
from contextlib import ExitStack

import numpy as np

import concourse.bass as bass
from concourse import mybir

F32 = mybir.dt.float32
BF16 = mybir.dt.bfloat16
I32 = mybir.dt.int32
U32 = mybir.dt.uint32
ALU = mybir.AluOpType
ACT = mybir.ActivationFunctionType
AX = mybir.AxisListType.X

P = 128
C = 128
IMGS, H, W = 2, 128, 128
M = IMGS * H * W
NH, DK, WS, SS = 8, 16, 8, 4
L = WS * WS
NWIN = W // WS
STRIPS = IMGS * H // WS
STOK = WS * W
HTOK = STOK // 2
REL = (2 * WS - 1) ** 2
EDGES = 524288
EC = EDGES // P
TC = M // P
MERGED = EDGES + M
GH, NE = 4, 4
GC = GH * NE
ROW = GC + 2 * GH
FF = 256
SRC_BITS = 15
KEY_BASE = 256
U = 64
BIG = 1.0e30
LN_C_EPS, LN_T_EPS, DEN_EPS = 1e-6, 1e-5, 1e-16

CONST = {}
_at = 0
for _name, _n in (("ident", P), ("center", P), ("mean", P), ("upper", P), ("ones", P), ("even", 1), ("odd", 1),
                  ("pair_even", 1), ("pair_odd", 1),
                  ("sign", 9), ("iota", 256), ("shift_mask", 4 * L), ("row_base", 2), ("earlier", 16)):
    CONST[_name] = (_at, _at + _n)
    _at += _n
CONST_COLS = _at


def constants():
    c = np.zeros((P, CONST_COLS), np.float32)

    def put(name, value):
        a, b = CONST[name]
        c[:, a:b] = value

    p = np.arange(P)
    put("ident", np.eye(P))
    put("center", np.eye(P) - 1.0 / P)
    put("mean", np.full((P, P), 1.0 / P))
    put("upper", p[:, None] <= p[None, :])
    put("ones", 1.0)
    scale = DK ** -0.5
    put("even", np.where((p // DK) % 2 == 0, scale, 0.0)[:, None])
    put("odd", np.where((p // DK) % 2 == 1, scale, 0.0)[:, None])
    put("pair_even", ((p // (2 * DK)) % 2 == 0)[:, None])
    put("pair_odd", ((p // (2 * DK)) % 2 == 1)[:, None])
    put("sign", np.where((p[:, None] >> np.arange(9)) & 1, -1.0, 1.0))
    put("iota", np.arange(256)[None, :])
    i, j = np.arange(L) // WS, np.arange(L) % WS
    masks = np.zeros((4, L, L), np.float32)
    for kind in range(4):
        region = (i >= WS - SS) * (2 * (kind // 2)) + (j >= WS - SS) * (kind % 2)
        masks[kind] = np.where(region[:, None] != region[None, :], -100.0, 0.0)
    put("shift_mask", np.tile(masks.transpose(1, 0, 2).reshape(L, 4 * L), (2, 1)))
    put("row_base", np.stack([p * EC - 1, EDGES + p * TC - 1], 1))
    put("earlier", (np.arange(NE)[None, :] < np.arange(NE)[:, None]).reshape(1, NE * NE))
    return c


def relative_one_hot():
    co = np.stack(np.meshgrid(np.arange(WS), np.arange(WS), indexing="ij")).reshape(2, -1)
    rel = co[:, :, None] - co[:, None, :] + (WS - 1)
    idx = rel[0] * (2 * WS - 1) + rel[1]
    out = np.zeros((REL, L, L), np.float32)
    t, s = np.meshgrid(np.arange(L), np.arange(L), indexing="ij")
    out[idx[t, s], s, t] = 1.0
    return out.reshape(REL, L * L)


N_LOADS = 18
ROUNDS = STRIPS + 2
GROUPS = 8
QUADS = 8
DEEP = 4
UNROLL = 3
USES = 10
FIRST_ALL = 2
FIRST_TURN = 8
LEVELS = 8
SLOTS = 4
SLOT_WEIGHT = (1.1, 1.0, 1.8, 2.0)


def slot_of(t, q):
    return SLOTS * t + q


def share(count, slot, first, last):
    def weight(i):
        early = 4 if i == 0 else 1.3 if SLOTS <= i < 2 * SLOTS else 1
        return SLOT_WEIGHT[i % SLOTS] * early

    total = sum(weight(i) for i in range(first, last + 1))
    before = sum(weight(i) for i in range(first, slot))
    return round(count * before / total), round(count * (before + weight(slot)) / total)


def partition_network():
    steps, blk = [], 2
    while blk <= EC:
        dist = blk // 2
        while dist:
            steps.append((dist, None if blk == EC else blk))
            dist //= 2
        blk *= 2
    return steps


OPEN = 4


class Done:

    def __init__(self, eng, semaphore, start=0):
        self.eng, self.sem, self.n = eng, semaphore, start

    def step(self, ins):
        ins.then_inc(self.sem, 1)
        self.n += 1

    def settle(self):
        self.eng.wait_ge(self.sem, self.n)


def program(nc, x, wq_t, bq, wkv_t, bkv, wproj_t, bproj, bias_table, w_gat, att_src, att_dst, b_gat, ln_gamma,
            ln_beta, w1, b1, w2, b2, edges, const, rel_hot, out):
    node_rows = nc.dram_tensor("node_rows", (M, ROW), F32, kind="Internal").ap()
    edge_rows = nc.dram_tensor("edge_rows", (MERGED, ROW), F32, kind="Internal").ap()
    x1_dram = nc.dram_tensor("x1_dram", (C, M), F32, kind="Internal").ap()
    xn_dram = nc.dram_tensor("xn_dram", (C, M), F32, kind="Internal").ap()
    y_dram = nc.dram_tensor("y_dram", (M // P, P, NE * C), F32, kind="Internal").ap()

    with ExitStack() as ctx:
        scopes = [ctx]

        def sb(name, shape, dt=F32):
            return scopes[-1].enter_context(nc.sbuf_tensor(name, shape, dt))

        def sem(name):
            return ctx.enter_context(nc.semaphore(name))

        bank = ctx.enter_context(nc.psum_tensor("bank", [P, 8, 512], F32))
        cst = sb("cst", [P, CONST_COLS])

        def con(name):
            return cst[:, CONST[name][0]:CONST[name][1]]

        keys = [sb("key_a", [P, EC + TC]), sb("key_b", [P, EC + TC])]
        dst_f = sb("dst_f", [P, EC + TC + 2])
        vec = sb("vec", [C, 9])
        att_s = sb("att_s", [P, 2 * GC])
        gate_s = sb("gate_s", [P, 3 * GC])
        eps = sb("eps", [P, 2])
        sign_now = sb("sign_now", [P, 1])
        wgat_s = sb("wgat_s", [C, GC])

        loaded = sem("loaded")
        vec_sums = sem("vec_sums")
        setup_done = sem("setup_done")
        edges_loaded = sem("edges_loaded")
        keys_made = sem("keys_made")
        self_loops = sem("self_loops")
        key_step = sem("key_step")
        turn_asked = sem("turn_asked")
        turned = sem("turned")
        turned_copy = sem("turned_copy")
        sorted_ = sem("sorted")

        evac = [sem(f"evac{b}") for b in range(2)]
        full = [sem(f"full{b}") for b in range(2)]
        x_loaded = [sem(f"x_loaded{b}") for b in range(UNROLL)]
        rstd_ready = sem("rstd_ready")
        xn_done = sem("xn_done")
        s_full = sem("s_full")
        biased = sem("biased")
        max_ready = sem("max_ready")
        centered = sem("centered")
        exp_ready = sem("exp_ready")
        inv_ready = sem("inv_ready")
        probs_ready = sem("probs_ready")
        pt_full = [sem(f"pt_full{b}") for b in range(2)]
        pt_evac = [sem(f"pt_evac{b}") for b in range(2)]
        strip_stored = [sem(f"strip_stored{b}") for b in range(UNROLL)]
        strip_saved = sem("strip_saved")
        node_done = sem("node_done")
        dve_own = sem("dve_own")

        vb_zero = sem("vb_zero")
        join_step = sem("join_step")
        chunk_step = sem("chunk_step")
        hot_ready = sem("hot_ready")
        counted = sem("counted")
        count_added = sem("count_added")
        y_full = [sem(f"y_full{b}") for b in range(2)]
        y_evac = [sem(f"y_evac{b}") for b in range(2)]
        y_stored = sem("y_stored")
        y_saved = sem("y_saved")
        up_full = sem("up_full")
        hidden = sem("hidden")
        first_got = sem("first_got")
        idx_ready = sem("idx_ready")
        gathered = [sem(f"gathered{b}") for b in range(2)]
        diff_ready = sem("diff_ready")
        weights_ready = sem("weights_ready")
        edge_used = sem("edge_used")
        rows_done = sem("rows_done")
        rows_stored = sem("rows_stored")
        rows_saved = sem("rows_saved")
        experts_loaded = sem("experts_loaded")
        xm_loaded = [sem(f"xm_loaded{b}") for b in range(2)]
        prefix_full = sem("prefix_full")
        chain_ready = sem("chain_ready")
        chain_turned = sem("chain_turned")
        chain_diff = sem("chain_diff")
        chain_exp = sem("chain_exp")
        run_got = sem("run_got")
        runs_joined = sem("runs_joined")
        run_put = sem("run_put")
        got_landed = [sem(f"got_landed{b}") for b in range(2)]
        idx_d_ready = sem("idx_d_ready")
        idx_taken = sem("idx_taken")
        gate_step = sem("gate_step")
        gate_asks = sem("gate_asks")
        gate_asks2 = sem("gate_asks2")
        gate_std = sem("gate_std")
        gate_exp = sem("gate_exp")
        gates_ready = sem("gates_ready")
        yo_loaded = [sem(f"yo_loaded{b}") for b in range(DEEP)]
        res_loaded = [sem(f"res_loaded{b}") for b in range(DEEP)]
        diag_dve = sem("diag_dve")
        diag_act = sem("diag_act")
        mixed = sem("mixed")
        fin_ready = sem("fin_ready")
        fin_saved = sem("fin_saved")
        out_stored = [sem(f"out_stored{b}") for b in range(DEEP)]

        scratch_i = sb("scratch_i", [P, 2 * (EC + TC)], I32)
        edge_i = scratch_i[:, 0:2 * EC].rearrange("p (a f) -> p a f", a=2)
        run_flag = scratch_i[:, 0:EC].bitcast(F32)
        first_row_i = sb("first_row_i", [P, 2], I32)
        end_i = sb("end_i", [P, 256], I32)
        bias = sb("bias", [P, 4, NH // 2, L])
        wq_s = sb("wq_s", [C, C])
        wkv_s = sb("wkv_s", [C, 2 * C])
        wproj_s = sb("wproj_s", [C, C])
        loops_i = sb("loops_i", [P, 2, 32, 8], I32)
        tails = [sb("tail_a", [P, 256]), sb("tail_b", [P, 256])]

        setup = ExitStack()
        scopes.append(setup)
        hot = sb("hot", [P, 2, L * L])
        table_s = sb("table_s", [P, 2, NH])
        scopes.pop()
        setup.close()

        stage_b = ExitStack()
        scopes.append(stage_b)
        prob = [sb(f"prob{g}", [P, 8, NH // 2, L]) for g in range(2)]
        pt = sb("pt", [P, 8, 2, P])
        vb = sb("vb", [P, NWIN, 2, 2, L])
        parts = [scratch_i[:, STOK * n:STOK * n + STOK].bitcast(F32) for n in range(2 * UNROLL)]
        xt = [a.rearrange("c (i w) -> c i w", w=W) for a in parts[:UNROLL]]
        xw = [a.rearrange("c (w i j) -> c w i j", i=WS, j=WS) for a in parts[UNROLL:]]
        xc = [sb(f"xc{n}", [C, 2, HTOK]) for n in range(2)]
        sq = [dst_f[:, 2 * HTOK * n:2 * HTOK * n + 2 * HTOK].rearrange("c (j t) -> c j t", j=2) for n in range(2)]
        rstd = [dst_f[:, 2 * HTOK * n:2 * HTOK * n + 2 * HTOK].rearrange("c (j t) -> c j t", j=2)
                for n in range(2, 4)]
        node_att = dst_f[:, 8 * HTOK:8 * HTOK + 16 * GC].rearrange("p (j r a) -> p j r a", j=2, r=4)
        q2 = sb("q2", [C, NWIN, 2, L])
        k2 = sb("k2", [C, NWIN, 2, L])
        row_max = sb("row_max", [P, 2, 8, NH // 2])
        row_sum = sb("row_sum", [P, 2, 8, NH // 2])
        row_inv = sb("row_inv", [P, 2, 8, NH // 2])
        ot = sb("ot", [C, NWIN, WS, WS])
        x1 = [sb(f"x1{b}", [C, WS, W]) for b in range(UNROLL)]
        x2 = [sb(f"x2{b}", [C, WS, W]) for b in range(UNROLL)]
        node = [sb(f"node{b}", [P, WS, ROW]) for b in range(UNROLL)]
        scopes.pop()
        stage_b.close()

        stage_c = ExitStack()
        scopes.append(stage_c)
        gath = [sb(f"gath{b}", [P, U, ROW]) for b in range(2)]
        idx = [sb(f"idx{b}", [P, U], I32) for b in range(2)]
        hilo_i = sb("hilo_i", [P, 2, U], I32)
        hilo = sb("hilo", [P, 2, U])
        iota_b = sb("iota_b", [P, 256], BF16)
        hot_b = [sb(f"hot_b{b}", [P, 8, 384], BF16) for b in range(2)]
        count = sb("count", [P, 256])
        new4 = sb("new4", [P, GH, U])
        keep4 = sb("keep4", [P, GH, U + 1])
        mask4 = sb("mask4", [P, GH, U + 1])
        adst_in = sb("adst_in", [P, GH, U + 1])
        adst = sb("adst", [P, GH, U + 1])
        logit = sb("logit", [P, GH, U + 1])
        leaky = sb("leaky", [P, GH, U + 1])
        run_max = sb("run_max", [P, GH, U + 1])
        diff = sb("diff", [P, 2, GH, U + 1])
        weight = sb("weight", [P, 2, GH, U + 1])
        terms = sb("terms", [P, NE, GH, U + 1])
        sums = sb("sums", [P, 1 + NE, GH, U + 1])
        first = [sb(f"first{n}", [P, ROW]) for n in range(2)]
        rows = [sb(f"rows{b}", [P, U, ROW]) for b in range(2)]
        ends = sb("ends", [P, 2, ROW])
        w1_s = sb("w1_s", [C, NE, FF])
        w2_s = sb("w2_s", [P, NE, 2, C])
        b1_s = sb("b1_s", [P, NE, 2])
        b2_s = sb("b2_s", [P, NE, C])
        xm = [sb(f"xm{b}", [C, 512]) for b in range(2)]
        hid = scratch_i[:, EC + TC:EC + TC + NE * 2 * 512].bitcast(F32).rearrange("p (k t) -> p k t", t=512)
        yt = [scratch_i[:, 2048 * b:2048 * b + 2048].bitcast(F32).rearrange("p (t f) -> p t f", t=4)
              for b in range(2)]
        run_len = sb("run_len", [P, 2])
        row_i = sb("row_i", [P, 2], I32)
        chain_in = sb("chain_in", [P, 2, 4, 20])
        chain = sb("chain", [20, 4, 257])
        ck = sb("ck", [20, 6, 257])
        joined = sb("joined", [20, 2, 256])
        carry = sb("carry", [P, 2, 2, 20])
        at_run = sb("at_run", [P, 2, ROW])
        jw = sb("jw", [P, 3, 2, 4])
        end_f = sb("end_f", [P, 256])
        tot = sb("tot", [P, 2, 256])
        scopes.pop()
        stage_c.close()

        stage_d = ExitStack()
        scopes.append(stage_d)
        idx_d = [sb(f"idx_d{b}", [P, 32], I32) for b in range(2)]
        got = [sb(f"got{b}", [P, 32, ROW]) for b in range(2)]
        sc = sb("sc", [P, 4, 32, GC])
        s1 = sb("s1", [P, 8, 32])
        s4 = sb("s4", [P, 6, 32, NE])
        gates = [sb(f"gates{b}", [P, 32, NE]) for b in range(2)]
        diag = [sb(f"diag{b}", [P, 4, NE, P]) for b in range(DEEP)]
        res = [sb(f"res{b}", [C, 512]) for b in range(DEEP)]
        yo = [sb(f"yo{b}", [P, 4, NE * C]) for b in range(DEEP)]
        fin = [sb(f"fin{b}", [C, 512]) for b in range(DEEP)]
        scopes.pop()
        stage_d.close()

        block = ctx.enter_context(nc.Block())

        def key(k):
            return keys[k][:, 0:EC]

        def exchange(d, src, dst, dist, blk):
            e = d.eng
            d.settle()
            if blk is None:
                s = src.rearrange("p (b t i) -> p b t i", t=2, i=dist)
                o = dst.rearrange("p (b t i) -> p b t i", t=2, i=dist)
                pairs = [(s[:, :, 0], s[:, :, 1], o[:, :, 0], o[:, :, 1])]
            else:
                n = blk // (2 * dist)
                s = src.rearrange("p (b r s t i) -> p r t b s i", r=2, t=2, i=dist, s=n)
                o = dst.rearrange("p (b r s t i) -> p r t b s i", r=2, t=2, i=dist, s=n)
                pairs = [(s[:, 0, 0], s[:, 0, 1], o[:, 0, 0], o[:, 0, 1]),
                         (s[:, 1, 0], s[:, 1, 1], o[:, 1, 1], o[:, 1, 0])]
            for lower, upper, small, large in pairs:
                d.step(e.tensor_tensor(small, lower, upper, ALU.min))
                d.step(e.tensor_tensor(large, lower, upper, ALU.max))

        def dve_setup(d):
            e = d.eng
            d.step(e.memset(eps[:, 0:1], LN_C_EPS))
            d.step(e.memset(eps[:, 1:2], LN_T_EPS))
            d.step(e.tensor_scalar(vec[:, 4:5], vec[:, 0:1], con("even"), None, ALU.mult))
            d.step(e.tensor_scalar(vec[:, 5:6], vec[:, 0:1], con("odd"), None, ALU.mult))
            d.step(e.tensor_scalar(vec[:, 7:8], vec[:, 1:2], con("pair_even"), None, ALU.mult))
            d.step(e.tensor_scalar(vec[:, 8:9], vec[:, 1:2], con("pair_odd"), None, ALU.mult))
            e.wait_ge(vec_sums, 2)
            d.step(e.tensor_tensor(vec[:, 6:7], bank[:, 1, 0:1], vec[:, 3:4], ALU.add))
            table = bank[:, 0, :].rearrange("p (s h) -> p h s", h=NH)
            mask = con("shift_mask").rearrange("p (k s) -> p k s", k=4)
            for half in range(2):
                rws = slice(64 * half, 64 * half + 64)
                for kind in range(4):
                    d.step(e.tensor_tensor(bias[rws, kind], table[rws, half::2, :],
                                           mask[rws, kind:kind + 1, :].broadcast_to([64, NH // 2, L]), ALU.add))

            d.settle()
            e.sem_inc(setup_done, 1)

        def make_keys(d):
            e = d.eng
            e.wait_ge(edges_loaded, 32)
            xor = keys[1][:, 0:EC].bitcast(I32)
            base = keys[0][:, 0:EC].bitcast(I32)
            d.step(e.tensor_tensor(xor, edge_i[:, 0, :], edge_i[:, 1, :], ALU.bitwise_xor))
            d.step(e.tensor_scalar(base, edge_i[:, 1, :], float(KEY_BASE), None, ALU.add))
            d.settle()
            d.step(e.scalar_tensor_tensor(edge_i[:, 0, :], base, SRC_BITS, xor, ALU.logical_shift_left,
                                          ALU.bitwise_or))
            e.wait_ge(self_loops, 1)
            d.step(e.tensor_scalar(loops_i[:, 1], loops_i[:, 0], SRC_BITS, None, ALU.logical_shift_left))
            d.settle()
            d.step(e.tensor_scalar(key(0), edge_i[:, 0, :].bitcast(F32), con("sign")[:, 0:1], None, ALU.mult))
            d.settle()
            e.sem_inc(keys_made, 1)

        def first_cross_step(d, level):
            e = d.eng
            dist = 1 << (level - 1)
            s, o = key(0), key(1)
            d.settle()
            if level == 7:
                s = s.rearrange("p (b t i) -> p b t i", t=2, i=dist)
                o = o.rearrange("p (b t i) -> p b t i", t=2, i=dist)
                pairs = [(s[:, :, 0], s[:, :, 1], o[:, :, 0], o[:, :, 1])]
            else:
                s = s.rearrange("p (b r t i) -> p r t b i", r=2, t=2, i=dist)
                o = o.rearrange("p (b r t i) -> p r t b i", r=2, t=2, i=dist)
                pairs = [(s[:, 0, 0], s[:, 0, 1], o[:, 0, 0], o[:, 0, 1]),
                         (s[:, 1, 0], s[:, 1, 1], o[:, 1, 1], o[:, 1, 0])]
            for lower, upper, small, large in pairs:
                d.step(e.scalar_tensor_tensor(small, upper, -1.0, lower, ALU.mult, ALU.min))
                d.step(e.scalar_tensor_tensor(large, upper, -1.0, lower, ALU.mult, ALU.max))

        def join_self_loops(d):
            e = d.eng
            last = key(0).rearrange("p (h b q) -> p h b q", b=2, q=P)[:, :, :, P - 8:P]
            loops = loops_i[:, 1].bitcast(F32).rearrange("p (h b) q -> p h b q", b=2)
            large, small = (t[:, :].rearrange("p (b q h) -> p h b q", b=2, q=8) for t in tails)
            d.step(e.tensor_tensor(large, last, loops, ALU.max))
            d.step(e.tensor_tensor(small, last, loops, ALU.min))
            d.settle()
            d.step(e.tensor_copy(last, small))

        def await_turn(e, n):
            e.wait_ge(turned_copy, 8 * n + 8 + OPEN)

        def ask_turn(d):
            d.settle()
            d.eng.sem_inc(turn_asked, 1)

        def sort_slot(d, t, q):
            e = d.eng
            at = slot_of(t, q)
            asks = [slot_of(FIRST_TURN + UNROLL * n, 2) for n in range(LEVELS + 1)]
            if at <= asks[0]:
                steps = partition_network()
                a, b = share(len(steps), at, 0, asks[0])
                for n in range(a, b):
                    exchange(d, key(n % 2), key(1 - n % 2), *steps[n])
                if at == asks[0]:
                    ask_turn(d)
                return
            if at > asks[-1]:
                return
            level = next(n for n in range(1, LEVELS + 1) if at <= asks[n])
            begun = asks[level - 1]
            if at <= begun + 3:
                if at == begun + 1:
                    await_turn(e, 2 * level - 2)
                    if level < 8:
                        first_cross_step(d, level)
                    else:
                        join_self_loops(d)
                if level < 8:
                    dists = [1 << n for n in range(level - 2, -1, -1)]
                    blk, cur = (None if level == 7 else 1 << level), 1
                else:
                    dists, blk, cur = [P // 2 >> n for n in range(7)], None, 0
                a, b = share(len(dists), at, begun + 1, begun + 3)
                for n in range(a, b):
                    exchange(d, key((cur + n) % 2), key((cur + n + 1) % 2), dists[n], blk)
                if at == begun + 3:
                    if level == 8:
                        d.settle()
                        d.step(e.tensor_copy(key(0), key(1)))
                    d.step(e.tensor_copy(sign_now[:, :], con("sign")[:, level:level + 1]))
                    ask_turn(d)
                return
            if at == begun + 5:
                await_turn(e, 2 * level - 1)
                if level == 8:
                    for n, dist in enumerate((64, 32, 16, 8, 4, 2, 1, 128)):
                        exchange(d, tails[n % 2][:, :], tails[1 - n % 2][:, :], dist, None)
                    ask_turn(d)
            if at < begun + 5:
                return
            a, b = share(12, at, begun + 5, asks[level])
            for n in range(a, b):
                exchange(d, key(n % 2), key(1 - n % 2), EC // 2 >> n, None)
            if at == asks[level] and level < LEVELS:
                ask_turn(d)

        def finish_sort(d):
            e = d.eng
            e.wait_ge(turned_copy, 8 * 2 * LEVELS + 1 + OPEN)
            for n in range(7):
                exchange(d, tails[1 - n % 2][:, :], tails[n % 2][:, :], P // 2 >> n, None)
            d.settle()
            d.step(e.tensor_copy(keys[0][:, EC:], tails[0][:, :]))
            k = keys[0][:, :].bitcast(I32)
            raw, dst_i = scratch_i[:, 0:EC + TC], scratch_i[:, EC + TC:]
            d.settle()
            d.step(e.tensor_scalar(raw, k, SRC_BITS, None, ALU.logical_shift_right))
            d.settle()
            d.step(e.tensor_scalar(dst_i, raw, -float(KEY_BASE), None, ALU.add))
            d.settle()
            d.step(e.scalar_tensor_tensor(keys[1][:, :].bitcast(I32), k, (1 << SRC_BITS) - 1, dst_i,
                                          ALU.bitwise_and, ALU.bitwise_xor))
            d.step(e.tensor_copy(first_row_i[:, 0:1], dst_i[:, 0:1]))
            d.step(e.tensor_copy(first_row_i[:, 1:2], dst_i[:, EC:EC + 1]))
            d.settle()
            e.sem_inc(sorted_, 1)

        def destinations(d):
            e = d.eng
            dst_i = scratch_i[:, EC + TC:]
            e.wait_ge(node_done, 2 * ROUNDS + OPEN)
            d.step(e.tensor_copy(dst_f[:, 1:1 + EC], dst_i[:, 0:EC]))
            d.step(e.tensor_copy(dst_f[:, 2 + EC:], dst_i[:, EC:]))
            d.settle()
            d.step(e.tensor_copy(dst_f[:, 0:1], dst_f[:, 1:2]))
            d.step(e.tensor_copy(dst_f[:, 1 + EC:2 + EC], dst_f[:, 2 + EC:3 + EC]))
            d.settle()

        def pass_over(e, semaphore, before, n):
            e.wait_ge(semaphore, before + OPEN)
            e.sem_inc(semaphore, n)

        def has(t):
            return 0 <= t < STRIPS, 0 <= t - 1 < STRIPS, 0 <= t - 2 < STRIPS

        def round_dve(e, t, d, own):
            _, has_n, has_c = has(t)
            par = (t - 2) % UNROLL

            def scores(g):
                if not has_n:
                    pass_over(e, biased, t * 3 + g, 1 + g)
                    pass_over(e, max_ready, t * 2 + g, 1)
                    return
                e.wait_ge(s_full, t * 2 + g + 1 + OPEN)
                e.wait_ge(pt_full[1], t * 4 + 2 * g + 2 + OPEN)
                kind = 2 * ((t - 1) % 16 // 15)
                sums = bank[:, 0:4, :].rearrange("p (a b) (w x) -> p a (b w) x", a=2, w=4)
                taken = prob[g][:, :, :, :].rearrange("p w (a b) s -> p a w (b s)", a=2)
                biases = bias[:, :].rearrange("p k (a b) s -> p a k (b s)", a=2)
                n = 8 - g
                e.tensor_tensor(taken[:, :, 0:n], sums[:, :, 0:n],
                                biases[:, :, kind:kind + 1].broadcast_to([P, 2, n, 2 * L]),
                                ALU.add).then_inc(biased, 1)
                if g:
                    e.tensor_tensor(taken[:, :, n:8], sums[:, :, n:8], biases[:, :, kind + 1:kind + 2],
                                    ALU.add).then_inc(biased, 1)
                e.wait_ge(biased, t * 3 + 1 + 2 * g + OPEN)
                e.tensor_reduce(row_max[:, g], prob[g][:, :, :, :], AX, ALU.max).then_inc(max_ready, 1)

            def inverse_sum(g):
                if not has_n:
                    pass_over(e, inv_ready, t * 2 + g, 1)
                    return
                e.wait_ge(exp_ready, t * 2 + g + 1 + OPEN)
                own.step(e.tensor_reduce(row_sum[:, g], prob[g][:, :, :, :], AX, ALU.add))
                own.settle()
                e.reciprocal(row_inv[:, g], row_sum[:, g]).then_inc(inv_ready, 1)

            scores(0)
            if t:
                sort_slot(d, t, 0)
            inverse_sum(0)
            if has_c:
                for j in range(2):
                    wait_full(e, t, 6 + j)
                    e.wait_ge(strip_saved, t - 3 + OPEN)
                    pr = bank[:, 6 + j, :].rearrange("p (i c) -> p i c", c=W)
                    rws = slice(4 * j, 4 * j + 4)
                    old = xt[par]
                    e.scalar_tensor_tensor(x1[par][:, rws, SS:W], pr[:, :, 0:W - SS], vec[:, 6:7],
                                           old[:, rws, SS:W], ALU.add, ALU.add)
                    e.scalar_tensor_tensor(x1[par][:, rws, 0:SS], pr[:, :, W - SS:W], vec[:, 6:7],
                                           old[:, rws, 0:SS], ALU.add, ALU.add).then_inc(evac[j], 1)
            sort_slot(d, t, 1)
            scores(1)
            sort_slot(d, t, 2)
            if has_c:
                for j in range(2):
                    wait_full(e, t, 18 + j)
                    nd = node[par][:, 4 * j:4 * j + 4, :]
                    e.tensor_copy(nd[:, :, 0:GC],
                                  bank[:, 6 + j, 0:4 * GC].rearrange("p (r c) -> p r c", c=GC)).then_inc(evac[j], 1)
                    wait_evac(e, t, 18 + j)
                    own.step(e.tensor_tensor(node_att[:, j].rearrange("p r (k c) -> p r k c", k=2),
                                             nd[:, :, 0:GC].unsqueeze(2).broadcast_to([P, 4, 2, GC]),
                                             att_s[:, :].rearrange("p (k c) -> p k c", k=2).unsqueeze(1)
                                             .broadcast_to([P, 4, 2, GC]), ALU.mult))
                    own.settle()
                    e.tensor_reduce(nd[:, :, GC:ROW], node_att[:, j].rearrange("p r (h e) -> p r h e", e=NE), AX,
                                    ALU.add).then_inc(node_done, 1)
            else:
                pass_over(e, node_done, t * 2, 2)
            inverse_sum(1)
            sort_slot(d, t, 3)

        def wait_evac(e, t, u):
            e.wait_ge(evac[u % 2], t * USES + u // 2 + 1 + OPEN)

        def wait_full(e, t, u):
            e.wait_ge(full[u % 2], t * USES + u // 2 + 1 + OPEN)

        def pe_setup(e):
            e.wait_ge(loaded, 16 * N_LOADS)
            rest = REL - P
            for s in range(L):
                for half in range(2):
                    for n, rws in enumerate((P, rest)):
                        last = e.matmul(bank[L * half:L * half + L, 0, NH * s:NH * s + NH],
                                        hot[0:rws, n, L * s:L * s + L], table_s[0:rws, n, :],
                                        start=n == 0, stop=n == 1)
            last.then_inc(vec_sums, 1)
            e.matmul(bank[:, 1, 0:1], wproj_s[:, :], vec[:, 2:3], start=True, stop=True).then_inc(vec_sums, 1)

        def turn_pe(e, t, n, src):
            for k in range(8):
                turn_eighth(e, t, n, src, k)

        def turn_eighth(e, t, n, src, k):
            if k == 0:
                e.wait_ge(turn_asked, n + 1 + OPEN)
            if k < 2:
                e.wait_ge(pt_evac[k], t * 4 + 4 + OPEN)
            else:
                e.wait_ge(turned_copy, n * 8 + k - 1 + OPEN)
            for q in range(4):
                part = slice(P * (4 * k + q), P * (4 * k + q) + P)
                m = e.transpose(bank[:, 4 + k % 2, P * q:P * q + P], src[:, part], con("ident"))
            m.then_inc(turned, 1)

        def turn_tail_pe(e, t):
            e.wait_ge(turn_asked, 2 * LEVELS + 1 + OPEN)
            e.wait_ge(pt_evac[0], t * 4 + 4 + OPEN)
            for b in range(2):
                m = e.transpose(bank[:, 4, P * b:P * b + P], tails[0][:, P * b:P * b + P], con("ident"))
            m.then_inc(turned, 1)

        def round_pe(e, t, k, strips, loads, turns=0, across=None, back=None):
            has_m, has_n, has_c = strips
            now, before, last = k, (k - 1) % UNROLL, (k - 2) % UNROLL

            def free(u):
                e.wait_ge(evac[u % 2], t * USES + u // 2 + OPEN)

            def skip(u):
                free(u)
                e.sem_inc(full[u % 2], 1)
                e.sem_inc(evac[u % 2], 1)

            def bk(u):
                return bank[:, 6 + u % 2, :]

            def center(u, source, j):
                e.matmul(bk(u), con("center"), source[:, 4 * j:4 * j + 4, :].rearrange("c i w -> c (i w)"),
                         start=True, stop=True).then_inc(full[u % 2], 1)

            def mean(u, n, j):
                e.matmul(bk(u), con("mean"), sq[n][:, j], start=True, stop=True).then_inc(full[u % 2], 1)

            def attend(g, u):
                if not has_c:
                    for b in range(2):
                        pass_over(e, pt_full[b], t * 4 + 2 * g, 2)
                        pass_over(e, pt_evac[b], t * 4 + 2 * g, 2)
                    skip(u)
                    return
                e.wait_ge(probs_ready, t * 2 + g - 1 + OPEN)
                for wp in range(5):
                    b = wp % 2
                    if wp < 4:
                        e.wait_ge(pt_evac[b], t * 4 + 2 * g + wp // 2 + OPEN)
                        for w in range(2):
                            for hh in range(2):
                                m = e.transpose(bank[:, 4 + b, P * (2 * w + hh):P * (2 * w + hh) + P],
                                                prob[g][:, 2 * wp + w, 2 * hh:2 * hh + 2, :]
                                                .rearrange("p k s -> p (k s)"), con("ident"))
                        m.then_inc(pt_full[b], 1)
                    if wp < 1:
                        continue
                    if wp == 1:
                        free(u)
                    e.wait_ge(pt_evac[(wp - 1) % 2], t * 4 + 2 * g + (wp - 1) // 2 + 1 + OPEN)
                    for w in (2 * wp - 2, 2 * wp - 1):
                        for hh in range(2):
                            for v in range(2):
                                m = e.matmul(bank[64 * hh:64 * hh + 64, 6 + u % 2, L * w:L * w + L],
                                             vb[:, 8 * g + w, hh, v, :], pt[:, w, hh, 64 * v:64 * v + 64],
                                             start=v == 0, stop=v == 1)
                m.then_inc(full[u % 2], 1)

            def score(g):
                if not has_n:
                    pass_over(e, s_full, t * 2 + g, 1)
                    return
                e.wait_ge(biased, t * 3 + g + OPEN)
                for w in range(8):
                    for half in range(2):
                        rws = slice(64 * half, 64 * half + 64)
                        m = e.matmul(bank[:, 2 * half + w // 4, P * (w % 4):P * (w % 4) + P],
                                     q2[rws, 8 * g + w].rearrange("c v t -> c (v t)"),
                                     k2[rws, 8 * g + w].rearrange("c k s -> c (k s)"), start=True, stop=True)
                m.then_inc(s_full, 1)

            for b in range(2):
                free(b)
            if not isinstance(turns, int) or turns:
                e.wait_ge(turned_copy, 8 * turns + OPEN)
            attend(0, 0)
            score(0)
            for j in range(2):
                if has_m:
                    free(1 + j)
                    e.wait_ge(x_loaded[now], 32 * loads)
                    center(1 + j, xt[now], j)
                else:
                    skip(1 + j)
            attend(1, 3)
            for j in range(2):
                if has_m:
                    wait_evac(e, t, 1 + j)
                    free(4 + j)
                    mean(4 + j, 0, j)
                else:
                    skip(4 + j)
            for j in range(2):
                if has_c:
                    if j == 0:
                        wait_evac(e, t, 0)
                        wait_evac(e, t, 3)
                    free(6 + j)
                    e.matmul(bk(6 + j), wproj_s[:, :],
                             ot[:, :, 4 * j:4 * j + 4, :].rearrange("c w i j -> c i w j"),
                             start=True, stop=True).then_inc(full[j], 1)
                else:
                    skip(6 + j)
            score(1)
            for j in range(2):
                if has_c:
                    wait_evac(e, t, 6 + j)
                    center(8 + j, x1[last], j)
                else:
                    skip(8 + j)
            for g in range(2):
                if has_n:
                    free(10 + g)
                    for w in range(8):
                        if back is not None and w % 2 == 0:
                            turn_eighth(e, t, turns, back, 4 * g + w // 2)
                        win = xw[before][:, 8 * g + w].rearrange("c i j -> c (i j)")
                        for half in range(2):
                            m = e.matmul(bk(10 + g)[L * half:L * half + L, L * w:L * w + L], win,
                                         wkv_s[:, C:2 * C].rearrange("c (u k d) -> c k u d", k=2, d=2 * DK)[:, half],
                                         start=True, stop=True)
                    m.then_inc(full[g], 1)
                else:
                    skip(10 + g)
            for j in range(2):
                if has_c:
                    free(12 + j)
                    mean(12 + j, 1, j)
                else:
                    skip(12 + j)
            if has_m:
                e.wait_ge(xn_done, t * 4 + 2 + OPEN)
            for g in range(2):
                for n, wgt in enumerate((wq_s[:, :], wkv_s[:, 0:C])):
                    u = 14 + 2 * g + n
                    if has_m:
                        free(u)
                        e.matmul(bk(u), wgt, xw[now][:, 8 * g:8 * g + 8].rearrange("c w i j -> c (w i j)"),
                                 start=True, stop=True).then_inc(full[n], 1)
                    else:
                        skip(u)
            if across is not None:
                turn_pe(e, t, turns, across)
            for j in range(2):
                if has_c:
                    e.wait_ge(xn_done, t * 4 + 3 + j + OPEN)
                    free(18 + j)
                    for r in range(4):
                        m = e.matmul(bank[:, 6 + j, GC * r:GC * r + GC], x2[last][:, 4 * j + r, :], wgat_s[:, :],
                                     start=True, stop=True)
                    m.then_inc(full[j], 1)
                else:
                    skip(18 + j)

        def turn_act(e, n, back, eighths=range(8)):
            for k in eighths:
                e.wait_ge(turned, n * 8 + k + 1 + OPEN)
                part = slice(512 * k, 512 * k + 512)
                if back:
                    e.activation(key(0)[:, part], bank[:, 4 + k % 2, :], ACT.Copy,
                                 scale=sign_now[:, 0:1]).then_inc(turned_copy, 1)
                else:
                    e.activation(key(0)[:, part], bank[:, 4 + k % 2, :], ACT.Copy).then_inc(turned_copy, 1)

        def turn_tail_act(e):
            e.wait_ge(turned, 8 * 2 * LEVELS + 1 + OPEN)
            e.activation(tails[1][:, :], bank[:, 4, 0:256], ACT.Copy).then_inc(turned_copy, 1)

        def round_act(e, t, strips, turns=0, across=False, back=False):
            has_m, has_n, has_c = strips

            def copy_transposed(g):
                if not has_c:
                    return
                for wp in range(4):
                    b = wp % 2
                    e.wait_ge(pt_full[b], t * 4 + 2 * g + wp // 2 + 1 + OPEN)
                    e.activation(pt[:, 2 * wp:2 * wp + 2], bank[:, 4 + b, :].rearrange(
                        "p (w h t) -> p w h t", w=2, h=2), ACT.Copy).then_inc(pt_evac[b], 1)

            def copy_attention(g, u):
                if not has_c:
                    return
                wait_full(e, t, u)
                e.activation(ot[:, 8 * g:8 * g + 8], bank[:, 6 + u % 2, :].rearrange(
                    "p (w i j) -> p w i j", i=WS, j=WS), ACT.Copy).then_inc(evac[u % 2], 1)

            def centered_copy(n, u0):
                for j in range(2):
                    u = u0 + j
                    wait_full(e, t, u)
                    e.activation(sq[n][:, j], bank[:, 6 + u % 2, :], ACT.Square)
                    e.activation(xc[n][:, j], bank[:, 6 + u % 2, :], ACT.Copy).then_inc(evac[u % 2], 1)

            def log_variance(n, u0):
                for j in range(2):
                    u = u0 + j
                    wait_full(e, t, u)
                    e.activation(rstd[n][:, j], bank[:, 6 + u % 2, :], ACT.Ln,
                                 bias=eps[:, n:n + 1]).then_inc(evac[u % 2], 1)

            def inverse_std(n, u0):
                for j in range(2):
                    wait_evac(e, t, u0 + j)
                    e.activation(rstd[n][:, j], rstd[n][:, j], ACT.Exp, scale=-0.5).then_inc(rstd_ready, 1)

            def exponentials(g):
                if not has_n:
                    pass_over(e, exp_ready, t * 2 + g, 1)
                    return
                e.wait_ge(centered, t * 2 + g + 1 + OPEN)
                e.activation(prob[g][:, :, :, :], prob[g][:, :, :, :], ACT.Exp).then_inc(exp_ready, 1)

            copy_transposed(0)
            copy_attention(0, 0)
            if has_m:
                if not isinstance(t, int) or t > 0:
                    e.wait_ge(xn_done, t * 4 - 2 + OPEN)
                centered_copy(0, 1)
            copy_transposed(1)
            exponentials(0)
            copy_attention(1, 3)
            if has_m:
                log_variance(0, 4)
                inverse_std(0, 4)
            else:
                pass_over(e, rstd_ready, t * 4, 2)
            if has_c:
                e.wait_ge(xn_done, t * 4 + OPEN)
                centered_copy(1, 8)
            if has_n:
                for g in range(2):
                    if back:
                        turn_act(e, turns, True, range(4 * g, 4 * g + 4))
                    wait_full(e, t, 10 + g)
                    for half in range(2):
                        rws = slice(64 * half, 64 * half + 64)
                        src = bank[rws, 6 + g, :].rearrange("p (w v d) -> p v w d", v=2, d=DK)
                        for v in range(2):
                            dst = vb[rws, 8 * g:8 * g + 8, :, v, :].rearrange("p w h (k u d) -> p k u (w h) d",
                                                                              k=2, u=2)
                            a = e.activation(dst[:, half, v], src[:, v], ACT.Copy)
                    a.then_inc(evac[g], 1)
            if has_c:
                log_variance(1, 12)
                inverse_std(1, 12)
            else:
                pass_over(e, rstd_ready, t * 4 + 2, 2)
            if has_m:
                e.wait_ge(s_full, t * 2 + 2 + OPEN)
                for g in range(2):
                    wins = slice(8 * g, 8 * g + 8)
                    wait_full(e, t, 14 + 2 * g)
                    src = bank[:, 6, :].rearrange("p (w t) -> p w t", t=L)
                    e.activation(q2[:, wins, 0, :], src, ACT.Identity, bias=vec[:, 4:5], scale=con("even"))
                    e.activation(q2[:, wins, 1, :], src, ACT.Identity, bias=vec[:, 5:6],
                                 scale=con("odd")).then_inc(evac[0], 1)
                    wait_full(e, t, 15 + 2 * g)
                    src = bank[:, 7, :].rearrange("p (w t) -> p w t", t=L)
                    e.activation(k2[:, wins, 0, :], src, ACT.Identity, bias=vec[:, 7:8], scale=con("pair_even"))
                    e.activation(k2[:, wins, 1, :], src, ACT.Identity, bias=vec[:, 8:9],
                                 scale=con("pair_odd")).then_inc(evac[1], 1)
            exponentials(1)
            if across:
                turn_act(e, turns, False)

        def round_pool(e, t, k, strips):
            has_m, has_n, has_c = strips
            now, last = k, (k - 2) % UNROLL

            def subtract_max(g):
                if not has_n:
                    pass_over(e, centered, t * 2 + g, 1)
                    return
                e.wait_ge(max_ready, t * 2 + g + 1 + OPEN)
                pr = prob[g][:, :, :, :].rearrange("p w h s -> p (w h) s")
                e.tensor_tensor(pr, pr, row_max[:, g].rearrange("p w h -> p (w h)").unsqueeze(2)
                                .broadcast_to([P, 32, L]), ALU.subtract).then_inc(centered, 1)

            def divide_by_sum(g):
                if not has_n:
                    pass_over(e, probs_ready, t * 2 + g, 1)
                    return
                e.wait_ge(inv_ready, t * 2 + g + 1 + OPEN)
                pr = prob[g][:, :, :, :].rearrange("p w h s -> p (w h) s")
                e.tensor_tensor(pr, pr, row_inv[:, g].rearrange("p w h -> p (w h)").unsqueeze(2)
                                .broadcast_to([P, 32, L]), ALU.mult).then_inc(probs_ready, 1)

            subtract_max(0)
            divide_by_sum(0)
            for j in range(2):
                if not has_m:
                    pass_over(e, xn_done, t * 4 + j, 1)
                    continue
                e.wait_ge(rstd_ready, t * 4 + j + 1 + OPEN)
                if not isinstance(t, int) or t > 0:
                    e.wait_ge(full[1], t * USES - (USES - 6) + OPEN)
                a = xc[0][:, j].rearrange("c (i w) -> c i w", w=W)
                s = rstd[0][:, j].rearrange("c (i w) -> c i w", w=W)
                o = xw[now][:, :, 4 * j:4 * j + 4, :].rearrange("c w i j -> c i w j")
                mid = slice(SS, SS + (NWIN - 1) * WS)
                e.tensor_tensor(o[:, :, 0:NWIN - 1, :], a[:, :, mid].rearrange("c i (w j) -> c i w j", j=WS),
                                s[:, :, mid].rearrange("c i (w j) -> c i w j", j=WS), ALU.mult)
                e.tensor_tensor(o[:, :, NWIN - 1, 0:SS], a[:, :, W - SS:W], s[:, :, W - SS:W], ALU.mult)
                e.tensor_tensor(o[:, :, NWIN - 1, SS:WS], a[:, :, 0:SS], s[:, :, 0:SS],
                                ALU.mult).then_inc(xn_done, 1)
            subtract_max(1)
            for j in range(2):
                if not has_c:
                    pass_over(e, xn_done, t * 4 + 2 + j, 1)
                    continue
                e.wait_ge(rstd_ready, t * 4 + 3 + j + OPEN)
                e.wait_ge(strip_saved, t - 3 + OPEN)
                e.tensor_tensor(x2[last][:, 4 * j:4 * j + 4, :].rearrange("c i w -> c (i w)"), xc[1][:, j],
                                rstd[1][:, j], ALU.mult).then_inc(xn_done, 1)
            divide_by_sum(1)

        EPIECE = EC // U
        TPIECE = TC // U

        def piece_start(d, n):
            e = d.eng
            if n == 0:
                e.wait_ge(first_got, 32)
                for t in (keep4[:, :, 0:1], weight[:, 0, :, 0:1]):
                    d.step(e.memset(t, 0.0))
                d.step(e.memset(mask4[:, :, 0:1], -BIG))
                d.step(e.tensor_copy(iota_b[:, :], con("iota")))
                d.step(e.memset(count[:, :], 0.0))
            d.settle()
            if n:
                e.wait_ge(rows_done, (EPIECE if n == 1 else EPIECE + TPIECE) + OPEN)
                d.step(e.tensor_copy(ends[:, n - 1, 0:20].rearrange("p (q o) -> p q o", o=1),
                                     sums[:, :, :, U:U + 1].rearrange("p q h o -> p (q h) o")))
                d.step(e.tensor_copy(ends[:, n - 1, 20:24].rearrange("p (q o) -> p q o", o=1),
                                     run_max[:, :, U:U + 1]))
                d.settle()
            if n < 2:
                d.step(e.tensor_copy(adst[:, :, U:U + 1], first[n][:, GC + GH:ROW].unsqueeze(2)))
                d.step(e.memset(run_max[:, :, U:U + 1], -BIG))
                d.step(e.memset(sums[:, :, :, U:U + 1], 0.0))

        DVE_C = 23

        def chunk_dve(e, c, par, i, at, experts):
            base = c * DVE_C
            col, pad = at
            step = [0]

            def own(ins):
                step[0] += 1
                ins.then_inc(chunk_step, 1)

            def settle():
                e.wait_ge(chunk_step, base + step[0] + OPEN)

            k = keys[0][:, bass.ds(col, U)].bitcast(I32)
            own(e.tensor_scalar(hilo_i[:, 0], k, SRC_BITS + 7, None, ALU.logical_shift_right))
            own(e.tensor_scalar(hilo_i[:, 1], k, SRC_BITS, P - 1, ALU.logical_shift_right, ALU.bitwise_and))
            settle()
            own(e.tensor_scalar(hilo[:, 0], hilo_i[:, 0], -float(KEY_BASE // P), None, ALU.add))
            own(e.tensor_copy(hilo[:, 1], hilo_i[:, 1]))
            settle()
            for q in range(U // 8):
                e.wait_ge(counted, c * 8 + q - 1 + OPEN)
                hb = hot_b[q % 2]
                for j in range(8):
                    jj = 8 * q + j
                    e.tensor_scalar(hb[:, j, 0:P], iota_b[:, 0:P], hilo[:, 1, jj:jj + 1], None, ALU.is_equal)
                    h = e.tensor_scalar(hb[:, j, P:384], iota_b[:, :], hilo[:, 0, jj:jj + 1], None, ALU.is_equal)
                h.then_inc(hot_ready, 1)
            if experts:
                for t in range(4):
                    b = t % 2
                    e.wait_ge(y_full[b], c * 2 + t // 2 + 1 + OPEN)
                    e.wait_ge(y_saved, c - 1 + OPEN)
                    e.tensor_tensor(yt[par][:, t, :], bank[:, 2 + b, :],
                                    b2_s[:, :, :].rearrange("p e c -> p (e c)"), ALU.add).then_inc(y_evac[b], 1)
            now = dst_f[:, bass.ds(col + pad + 1, U)].unsqueeze(1).broadcast_to([P, GH, U])
            before = dst_f[:, bass.ds(col + pad, U)].unsqueeze(1).broadcast_to([P, GH, U])
            own(e.tensor_tensor(new4[:, :, :], now, before, ALU.not_equal))
            own(e.tensor_tensor(keep4[:, :, 1:], now, before, ALU.is_equal))
            settle()
            own(e.tensor_scalar(mask4[:, :, 1:], keep4[:, :, 1:], -1.0, BIG, ALU.add, ALU.mult))
            own(e.tensor_copy(adst_in[:, :, 0:1], adst[:, :, U:U + 1]))
            e.wait_ge(gathered[par], (i + 1) * (16 * U))
            g = gath[par][:, :, :].rearrange("p j r -> p r j")
            own(e.tensor_tensor(adst_in[:, :, 1:], new4[:, :, :], g[:, GC + GH:ROW], ALU.mult))
            settle()
            own(e.tensor_tensor_scan(flat(adst), flat(keep4), flat(adst_in), 0.0, ALU.mult, ALU.add))
            settle()
            own(e.tensor_tensor(logit[:, :, 1:], adst[:, :, 1:], g[:, GC:GC + GH], ALU.add))
            settle()
            own(e.scalar_tensor_tensor(leaky[:, :, 1:], logit[:, :, 1:], 0.2, logit[:, :, 1:], ALU.mult, ALU.max))
            own(e.tensor_copy(leaky[:, :, 0:1], run_max[:, :, U:U + 1]))
            e.wait_ge(rows_done, c + OPEN)
            settle()
            own(e.tensor_tensor_scan(flat(run_max), flat(mask4), flat(leaky), 0.0, ALU.add, ALU.max))
            settle()
            own(e.tensor_tensor(diff[:, 0, :, 1:], run_max[:, :, 0:U], mask4[:, :, 1:], ALU.add))
            own(e.tensor_tensor(diff[:, 1, :, 1:], leaky[:, :, 1:], run_max[:, :, 1:], ALU.subtract))
            settle()
            e.tensor_tensor(diff[:, 0, :, 1:], diff[:, 0, :, 1:], run_max[:, :, 1:],
                            ALU.subtract).then_inc(diff_ready, 1)
            own(e.tensor_copy(weight[:, 1, :, 0:1], sums[:, 0, :, U:U + 1]))
            own(e.tensor_copy(terms[:, :, :, 0:1], sums[:, 1:, :, U:U + 1]))
            e.wait_ge(weights_ready, c + 1 + OPEN)
            e.tensor_tensor(terms[:, :, :, 1:], weight[:, 1:2, :, 1:].broadcast_to([P, NE, GH, U]),
                            g[:, 0:GC].rearrange("p (h e) j -> p e h j", e=NE), ALU.mult).then_inc(edge_used, 1)
            e.wait_ge(edge_used, c + 1 + OPEN)
            settle()
            for q in range(1 + NE):
                data = flat3(weight[:, 1]) if q == 0 else flat3(terms[:, q - 1])
                own(e.tensor_tensor_scan(flat3(sums[:, q]), flat3(weight[:, 0]), data, 0.0, ALU.mult, ALU.add))
            settle()
            assert step[0] == DVE_C, step[0]
            e.wait_ge(counted, c * 8 + 8 + OPEN)
            e.wait_ge(count_added, c + OPEN)
            e.tensor_tensor(count[:, :], count[:, :], bank[:, 4 + par, 0:256], ALU.add).then_inc(count_added, 1)

        def flat(t):
            return t[:, :, :].rearrange("p h j -> p (h j)")

        def flat3(a):
            return a.rearrange("p h j -> p (h j)")

        def chunk_pe(e, c, par, i, experts):
            for q in range(U // 8):
                e.wait_ge(hot_ready, c * 8 + q + 1 + OPEN)
                if q == 0:
                    e.wait_ge(count_added, c - 1 + OPEN)
                hb = hot_b[q % 2]
                for j in range(8):
                    m = e.matmul(bank[:, 4 + par, 0:256], hb[:, j, 0:P], hb[:, j, P:384],
                                 start=q == 0 and j == 0, stop=q == U // 8 - 1 and j == 7)
                m.then_inc(counted, 1)
            if not experts:
                return
            e.wait_ge(xm_loaded[par], (i + 1) * 16)
            for k in range(2 * NE):
                e.wait_ge(hidden, c * 8 + k - 1 + OPEN)
                e.matmul(bank[:, k % 2, :], w1_s[:, k // 2, P * (k % 2):P * (k % 2) + P], xm[par][:, :],
                         start=True, stop=True).then_inc(up_full, 1)
            e.wait_ge(hidden, c * 8 + 8 + OPEN)
            for t in range(4):
                b = t % 2
                e.wait_ge(y_evac[b], c * 2 + t // 2 + OPEN)
                for k in range(2 * NE):
                    m = e.matmul(bank[:, 2 + b, C * (k // 2):C * (k // 2) + C], hid[:, k, P * t:P * t + P],
                                 w2_s[:, k // 2, k % 2, :], start=k % 2 == 0, stop=k % 2 == 1)
                m.then_inc(y_full[b], 1)

        def chunk_act(e, c, par, i, experts):
            if experts:
                e.wait_ge(y_full[1], c * 2 + OPEN)
                for k in range(2 * NE):
                    e.wait_ge(up_full, c * 8 + k + 1 + OPEN)
                    e.activation(hid[:, k, :], bank[:, k % 2, :], ACT.Gelu,
                                 bias=b1_s[:, k // 2, k % 2:k % 2 + 1]).then_inc(hidden, 1)
            e.wait_ge(diff_ready, c + 1 + OPEN)
            e.activation(weight[:, :, :, 1:].rearrange("p a h j -> p (a h) j"),
                         diff[:, :, :, 1:].rearrange("p a h j -> p (a h) j"), ACT.Exp).then_inc(weights_ready, 1)
            e.wait_ge(chunk_step, c * DVE_C + DVE_C + OPEN)
            e.wait_ge(rows_saved, c - 1 + OPEN)
            rw = rows[par][:, :, :].rearrange("p j r -> p r j")
            e.activation(rw[:, 0:20], sums[:, :, :, 1:].rearrange("p q h j -> p (q h) j"), ACT.Copy)
            e.activation(rw[:, 20:24], run_max[:, :, 1:], ACT.Copy).then_inc(rows_done, 1)

        def chunk_pool(e, c, par, i, col):
            e.wait_ge(edge_used, c - 1 + OPEN)
            e.tensor_copy(idx[par][:, :], keys[1][:, bass.ds(col, U)].bitcast(I32)).then_inc(idx_ready, 1)
            e.wait_ge(idx_ready, c + 1 + OPEN)
            e.sem_inc(idx_taken, 1)
            for j in range(U):
                e.indirect_dma_start(gath[par][:, j, :], None, node_rows,
                                     bass.IndirectOffsetOnAxis(ap=idx[par][:, j:j + 1].bitcast(U32), axis=0)
                                     ).then_inc(gathered[par], 16)

        def last_dst(n):
            return dst_f[:, EC:EC + 1] if n == 0 else dst_f[:, EC + TC + 1:]

        def first_dst(n):
            return dst_f[:, 1:2] if n == 0 else dst_f[:, EC + 2:EC + 3]

        def dve_run_rows(d):
            e = d.eng
            for n, (a, w) in enumerate(((1, EC), (EC + 2, TC))):
                d.step(e.tensor_scalar(run_flag[:, 0:w], dst_f[:, a:a + w], first_dst(n), None, ALU.is_equal))
                d.settle()
                d.step(e.tensor_reduce(run_len[:, n:n + 1], run_flag[:, 0:w], AX, ALU.add))
                d.settle()
            d.step(e.tensor_tensor(row_i[:, :], run_len[:, :], con("row_base"), ALU.add))

        def dve_join(d):
            e = d.eng
            e.wait_ge(prefix_full, 1)
            d.step(e.tensor_copy(tot[:, 0], bank[:, 7, 0:256]))
            d.settle()
            d.step(e.tensor_tensor_scan(tot[:, 1], tot[:, 0], tot[:, 0], 0.0, ALU.add, ALU.max))
            d.step(e.tensor_scalar(end_f[:, :], bank[:, 6, 0:256], -1.0, None, ALU.add))
            d.settle()
            d.step(e.tensor_tensor(end_f[:, :], end_f[:, :], tot[:, 1], ALU.add))
            d.settle()
            d.step(e.tensor_tensor(end_i[:, :], end_f[:, :], tot[:, 0], ALU.subtract))
            for n in range(2):
                d.step(e.tensor_copy(chain_in[:, n, 0].rearrange("p (q h) -> p q h", h=GH),
                                     ends[:, n, 20:24].unsqueeze(1).broadcast_to([P, 5, GH])))
                d.step(e.tensor_copy(chain_in[:, n, 1], ends[:, n, 0:20]))
                d.step(e.tensor_copy(chain_in[:, n, 2], last_dst(n).broadcast_to([P, 20])))
                d.step(e.tensor_copy(chain_in[:, n, 3], first_dst(n).broadcast_to([P, 20])))
            d.step(e.memset(chain[:, :, 0:1], -1.0))
            d.step(e.memset(ck[:, 0, 0:1], 0.0))
            d.step(e.memset(ck[:, 2, 0:1], -BIG))
            d.settle()
            e.sem_inc(chain_ready, 1)
            e.wait_ge(chain_turned, 1)
            d.step(e.tensor_copy(chain[:, :, 1:].rearrange("q k (n p) -> q n k p", n=2),
                                 bank[0:20, 0:2, :].rearrange("q n (k p) -> q n k p", k=4)))
            d.settle()
            big, den, last, frst = (chain[:, k, 1:] for k in range(4))
            prev_last = chain[:, 2, 0:256]
            keep, mask, diffs = ck[:, 1, 1:], ck[:, 5, 1:], ck[:, 3:5, 1:]
            d.step(e.tensor_tensor(keep, last, prev_last, ALU.is_equal))
            d.settle()
            d.step(e.tensor_scalar(mask, keep, -1.0, BIG, ALU.add, ALU.mult))
            d.settle()
            d.step(e.tensor_tensor_scan(ck[:, 2, 1:], mask, big, -BIG, ALU.add, ALU.max))
            d.settle()
            d.step(e.tensor_tensor(ck[:, 3, 1:], ck[:, 2, 0:256], mask, ALU.add))
            d.step(e.tensor_tensor(ck[:, 4, 1:], big, ck[:, 2, 1:], ALU.subtract))
            d.settle()
            d.step(e.tensor_tensor(ck[:, 3, 1:], ck[:, 3, 1:], ck[:, 2, 1:], ALU.subtract))
            d.settle()
            e.sem_inc(chain_diff, 1)
            e.wait_ge(chain_exp, 1)
            d.step(e.tensor_tensor(ck[:, 4, 1:], ck[:, 4, 1:], den, ALU.mult))
            d.step(e.tensor_tensor(ck[:, 5, 1:], frst, prev_last, ALU.is_equal))
            d.settle()
            d.step(e.tensor_tensor_scan(ck[:, 0, 1:], ck[:, 3, 1:], ck[:, 4, 1:], 0.0, ALU.mult, ALU.add))
            d.step(e.tensor_scalar(ck[:, 5, 1:], ck[:, 5, 1:], -1.0, BIG, ALU.add, ALU.mult))
            d.settle()
            d.step(e.tensor_tensor(joined[:, 0], ck[:, 2, 0:256], ck[:, 5, 1:], ALU.add))
            d.step(e.tensor_copy(joined[:, 1], ck[:, 0, 0:256]))
            d.settle()
            e.sem_inc(chain_ready, 1)
            e.wait_ge(chain_turned, 2)
            d.step(e.tensor_copy(carry[:, :, :, :].rearrange("p n k q -> p (n k q)"), bank[:, 2, 0:80]))
            e.wait_ge(run_got, 32)
            d.settle()
            rmax, rin = at_run[:, :, 20:24], carry[:, :, 0, 0:4]
            new, own_d, in_d = (jw[:, k] for k in range(3))
            d.step(e.tensor_tensor(new, rmax, rin, ALU.max))
            d.settle()
            d.step(e.tensor_tensor(own_d, rmax, new, ALU.subtract))
            d.step(e.tensor_tensor(in_d, rin, new, ALU.subtract))
            d.settle()
            e.sem_inc(chain_diff, 1)
            e.wait_ge(chain_exp, 2)
            sm = at_run[:, :, 0:20].rearrange("p n (q h) -> p n q h", h=GH)
            ci = carry[:, :, 1, :].rearrange("p n (q h) -> p n q h", h=GH)
            d.step(e.tensor_tensor(sm, sm, own_d.unsqueeze(2).broadcast_to([P, 2, 5, GH]), ALU.mult))
            d.step(e.tensor_tensor(ci, ci, in_d.unsqueeze(2).broadcast_to([P, 2, 5, GH]), ALU.mult))
            d.settle()
            d.step(e.tensor_tensor(sm, sm, ci, ALU.add))
            d.step(e.tensor_copy(rmax, new))
            d.settle()
            e.sem_inc(runs_joined, 1)

        def pe_join(e):
            e.wait_ge(count_added, EPIECE + TPIECE + OPEN)
            e.matmul(bank[:, 6, 0:256], con("upper"), count[:, :], start=True, stop=True)
            e.matmul(bank[:, 7, 0:256], con("ones"), count[:, :], start=True, stop=True).then_inc(prefix_full, 1)
            e.wait_ge(chain_ready, 1)
            for n in range(2):
                for k in range(4):
                    t = e.transpose(bank[0:20, n, P * k:P * k + P], chain_in[:, n, k, :], con("ident"))
            t.then_inc(chain_turned, 1)
            e.wait_ge(chain_ready, 2)
            for n in range(2):
                for k in range(2):
                    t = e.transpose(bank[:, 2, 20 * (2 * n + k):20 * (2 * n + k) + 20],
                                    joined[:, k, P * n:P * n + P], con("ident")[0:20, 0:20])
            t.then_inc(chain_turned, 1)

        def act_join(e):
            e.wait_ge(chain_diff, 1)
            e.activation(ck[:, 3:5, 1:], ck[:, 3:5, 1:], ACT.Exp).then_inc(chain_exp, 1)
            e.wait_ge(chain_diff, 2)
            e.activation(jw[:, 1:3], jw[:, 1:3], ACT.Exp).then_inc(chain_exp, 1)

        def pool_join(e):
            e.wait_ge(rows_saved, EPIECE + TPIECE + OPEN)
            for n in range(2):
                e.indirect_dma_start(at_run[:, n, :], None, edge_rows,
                                     bass.IndirectOffsetOnAxis(ap=row_i[:, n:n + 1].bitcast(U32), axis=0)
                                     ).then_inc(run_got, 16)
            e.wait_ge(run_got, 32)
            e.wait_ge(runs_joined, 1)
            for n in range(2):
                e.indirect_dma_start(edge_rows, bass.IndirectOffsetOnAxis(ap=row_i[:, n:n + 1].bitcast(U32), axis=0),
                                     at_run[:, n, :], None).then_inc(run_put, 16)
            e.wait_ge(run_put, 32)

        DVE_D = 21
        gate_n = [0]

        def gates_dve(e, g, par, got_count, part):
            base = g * DVE_D

            def own(ins):
                gate_n[0] += 1
                ins.then_inc(gate_step, 1)

            def settle():
                e.wait_ge(gate_step, base + gate_n[0] + OPEN)

            def each(v, shape):
                return v.unsqueeze(len(v.shape)).broadcast_to(shape)

            r = got[par][:, :, :]
            wide, nar = [P, 32, GC], [P, 32, NE]
            if part == 0:
                gate_n[0] = 0
                e.wait_ge(got_landed[par], got_count * (16 * 32))
                own(e.tensor_scalar(s4[:, 0], r[:, :, 0:GH], DEN_EPS, None, ALU.add))
                settle()
                own(e.reciprocal(s4[:, 1], s4[:, 0]))
                settle()
                own(e.tensor_tensor(sc[:, 0].rearrange("p n (h e) -> p n h e", e=NE),
                                    r[:, :, GH:20].rearrange("p n (e h) -> p n h e", h=GH),
                                    each(s4[:, 1], [P, 32, GH, NE]), ALU.mult))
                settle()
                own(e.tensor_tensor(sc[:, 0], sc[:, 0], gate_s[:, 0:GC].unsqueeze(1).broadcast_to(wide), ALU.add))
                settle()
                own(e.tensor_reduce(s1[:, 0], sc[:, 0], AX, ALU.add))
                settle()
                own(e.tensor_scalar(s1[:, 1], s1[:, 0], 1.0 / GC, None, ALU.mult))
                settle()
                own(e.tensor_tensor(sc[:, 1], sc[:, 0], each(s1[:, 1], wide), ALU.subtract))
                settle()
                own(e.tensor_tensor(sc[:, 2], sc[:, 1], sc[:, 1], ALU.mult))
                settle()
                e.tensor_reduce(s1[:, 2], sc[:, 2], AX, ALU.add).then_inc(gate_asks, 1)
            elif part == 1:
                e.wait_ge(gate_std, g * 2 + 2 + OPEN)
                own(e.tensor_tensor(sc[:, 2], sc[:, 1], each(s1[:, 3], wide), ALU.mult))
                settle()
                own(e.tensor_tensor(sc[:, 1], sc[:, 2], gate_s[:, GC:2 * GC].unsqueeze(1).broadcast_to(wide),
                                    ALU.mult))
                settle()
                own(e.tensor_tensor(sc[:, 2], sc[:, 1], gate_s[:, 2 * GC:].unsqueeze(1).broadcast_to(wide), ALU.add))
                settle()
                own(e.tensor_reduce(s4[:, 2], sc[:, 2].rearrange("p n (h e) -> p n e h", e=NE), AX, ALU.add))
                settle()
                own(e.tensor_reduce(s1[:, 5], s4[:, 2], AX, ALU.max))
                settle()
                e.tensor_tensor(s4[:, 3], s4[:, 2], each(s1[:, 5], nar), ALU.subtract).then_inc(gate_asks2, 1)
                mine = each(s4[:, 2], [P, 32, NE, NE])
                other = s4[:, 2].unsqueeze(2).broadcast_to([P, 32, NE, NE])
                gt, eq = (sc[:, k].rearrange("p n (e f) -> p n e f", f=NE) for k in (0, 1))
                own(e.tensor_tensor(gt, other, mine, ALU.is_gt))
                own(e.tensor_tensor(eq, other, mine, ALU.is_equal))
                settle()
                own(e.tensor_tensor(sc[:, 2], sc[:, 1], con("earlier").unsqueeze(1).broadcast_to(wide), ALU.mult))
            else:
                settle()
                own(e.tensor_tensor(sc[:, 1], sc[:, 0], sc[:, 2], ALU.add))
                settle()
                own(e.tensor_reduce(s4[:, 4], sc[:, 1].rearrange("p n (e f) -> p n e f", f=NE), AX, ALU.add))
                settle()
                e.wait_ge(gate_exp, g + 1 + OPEN)
                own(e.scalar_tensor_tensor(s4[:, 5], s4[:, 4], 1.5, s4[:, 3], ALU.is_lt, ALU.mult))
                settle()
                own(e.tensor_reduce(s1[:, 6], s4[:, 5], AX, ALU.add))
                settle()
                own(e.reciprocal(s1[:, 7], s1[:, 6]))
                settle()
                assert gate_n[0] == DVE_D, gate_n[0]
                e.tensor_tensor(gates[par][:, :, :], s4[:, 5], each(s1[:, 7], nar), ALU.mult).then_inc(gates_ready, 1)

        def diagonals_dve(e, g, par, k):
            n = g * QUADS + k
            e.wait_ge(mixed, n - DEEP + 1 + OPEN)
            e.tensor_tensor(diag[k % DEEP][:, 0:2], con("ident").unsqueeze(1).unsqueeze(1)
                            .broadcast_to([P, 2, NE, P]),
                            gates[par][:, 4 * k:4 * k + 2, :].unsqueeze(3).broadcast_to([P, 2, NE, P]),
                            ALU.mult).then_inc(diag_dve, 1)

        def group_dve(e, g, par, i, more):
            for k in range(QUADS):
                b = k % DEEP
                if k + 2 < QUADS:
                    diagonals_dve(e, g, par, k + 2)
                elif more:
                    if k + 2 == QUADS:
                        e.wait_ge(gates_ready, g + 2 + OPEN)
                    diagonals_dve(e, g + 1, 1 - par, k + 2 - QUADS)
                n = g * QUADS + k
                e.wait_ge(mixed, n + 1 + OPEN)
                e.wait_ge(res_loaded[b], g * (16 * QUADS // DEEP) + 16 * (k // DEEP + 1))
                e.wait_ge(fin_saved, n - DEEP + 1 + OPEN)
                e.tensor_tensor(fin[b][:, :], bank[:, b, :], res[b][:, :], ALU.add).then_inc(fin_ready, 1)
                if more and k in (1, 3, 5):
                    gates_dve(e, g + 1, 1 - par, i + 1 + par, k // 2)

        def group_pe(e, g):
            for k in range(QUADS):
                b = k % DEEP
                n = g * QUADS + k
                e.wait_ge(diag_dve, n + 1 + OPEN)
                e.wait_ge(diag_act, n + 1 + OPEN)
                e.wait_ge(yo_loaded[b], g * (16 * QUADS // DEEP) + 16 * (k // DEEP + 1))
                e.wait_ge(fin_ready, n - DEEP + 1 + OPEN)
                for h in range(4):
                    for ex in range(NE):
                        m = e.matmul(bank[:, b, P * h:P * h + P], yo[b][:, h, C * ex:C * ex + C],
                                     diag[b][:, h, ex, :], start=ex == 0, stop=ex == NE - 1)
                m.then_inc(mixed, 1)

        def gates_act(e, g, part):
            if part == 0:
                e.wait_ge(gate_asks, g + 1 + OPEN)
                e.activation(s1[:, 3], s1[:, 2], ACT.Ln, bias=eps[:, 1:2], scale=1.0 / GC).then_inc(gate_std, 1)
                e.wait_ge(gate_std, g * 2 + 1 + OPEN)
                e.activation(s1[:, 3], s1[:, 3], ACT.Exp, scale=-0.5).then_inc(gate_std, 1)
            else:
                e.wait_ge(gate_asks2, g + 1 + OPEN)
                e.activation(s4[:, 3], s4[:, 3], ACT.Exp, scale=1.0 / GH).then_inc(gate_exp, 1)

        def diagonals_act(e, g, par, k):
            e.wait_ge(mixed, g * QUADS + k - DEEP + 1 + OPEN)
            for h in (2, 3):
                for ex in range(NE):
                    a = e.activation(diag[k % DEEP][:, h, ex, :], con("ident"), ACT.Copy,
                                     scale=gates[par][:, 4 * k + h, ex:ex + 1])
            a.then_inc(diag_act, 1)

        def group_act(e, g, par, more):
            for k in range(QUADS):
                if k + 2 < QUADS:
                    diagonals_act(e, g, par, k + 2)
                elif more:
                    if k + 2 == QUADS:
                        e.wait_ge(gates_ready, g + 2 + OPEN)
                    diagonals_act(e, g + 1, 1 - par, k + 2 - QUADS)
                if more and k in (1, 3):
                    gates_act(e, g + 1, k // 2)

        def group_pool(e, g, par, i):
            e.wait_ge(gates_ready, g - 1 + OPEN)
            e.tensor_copy(idx_d[par][:, :], end_i[:, bass.ds(g * 32, 32)]).then_inc(idx_d_ready, 1)
            e.wait_ge(idx_d_ready, g + 1 + OPEN)
            e.sem_inc(idx_taken, 1)
            for j in range(32):
                e.indirect_dma_start(got[par][:, j, :], None, edge_rows,
                                     bass.IndirectOffsetOnAxis(ap=idx_d[par][:, j:j + 1].bitcast(U32), axis=0)
                                     ).then_inc(got_landed[par], 16)

        @block.vector
        def _(e):
            for t in (biased, max_ready, inv_ready, chunk_step, hot_ready, diff_ready,
                      edge_used, count_added, *y_evac, gate_step, gates_ready, diag_dve, fin_ready,
                      gate_asks, gate_asks2, turn_asked, node_done):
                e.sem_inc(t, OPEN)
            d = Done(e, key_step)
            own = Done(e, dve_own)
            e.wait_ge(loaded, 16 * N_LOADS)
            make_keys(d)
            sort_slot(d, 0, 0)
            dve_setup(d)
            for t in range(ROUNDS):
                round_dve(e, t, d, own)
            finish_sort(d)
            destinations(d)
            j = Done(e, join_step)
            e.wait_ge(strip_saved, STRIPS + OPEN)
            dve_run_rows(j)
            piece_start(j, 0)
            with e.Fori(0, EPIECE // 2) as i:
                for par in range(2):
                    chunk_dve(e, i * 2 + par, par, i, ((i * 2 + par) * U, 0), True)
            piece_start(j, 1)
            with e.Fori(EPIECE // 2, (EPIECE + TPIECE) // 2) as i:
                for par in range(2):
                    chunk_dve(e, i * 2 + par, par, i, ((i * 2 + par) * U, 1), False)
            piece_start(j, 2)
            dve_join(j)
            for part in range(3):
                gates_dve(e, 0, 0, 1, part)
            e.wait_ge(gates_ready, 1 + OPEN)
            for k in range(2):
                diagonals_dve(e, 0, 0, k)
            with e.Fori(0, GROUPS // 2 - 1) as i:
                for par in range(2):
                    group_dve(e, i * 2 + par, par, i, True)
            for g in range(GROUPS - 2, GROUPS):
                group_dve(e, g, g % 2, g // 2, g < GROUPS - 1)

        @block.tensor
        def _(e):
            for t in (*full, s_full, *pt_full, turned, counted, up_full, *y_full, mixed):
                e.sem_inc(t, OPEN)
            pe_setup(e)
            for t in range(FIRST_ALL):
                if t == 1:
                    e.wait_ge(setup_done, 1)
                round_pe(e, t, t, has(t), 1)
            with e.Fori(0, (FIRST_TURN - FIRST_ALL) // UNROLL) as i:
                for k in range(FIRST_ALL, FIRST_ALL + UNROLL):
                    round_pe(e, i * UNROLL + k, k % UNROLL, (True,) * 3, i + k // UNROLL + 1)
            with e.Fori(0, LEVELS // 2) as i:
                for level in range(2):
                    turns = i * 4 + 2 * level
                    for k, keyed in enumerate((dict(across=key(0)), dict(back=key(1 - level)), {})):
                        t = FIRST_TURN + UNROLL * level + k
                        round_pe(e, i * (2 * UNROLL) + t, t % UNROLL, (True,) * 3, i * 2 + t // UNROLL + 1,
                                 turns + k, **keyed)
            for t in range(STRIPS, ROUNDS):
                round_pe(e, t, t % UNROLL, has(t), None, 2 * LEVELS)
            turn_tail_pe(e, t)
            e.wait_ge(experts_loaded, 16 * 5)
            with e.Fori(0, EPIECE // 2) as i:
                for par in range(2):
                    chunk_pe(e, i * 2 + par, par, i, True)
            with e.Fori(EPIECE // 2, (EPIECE + TPIECE) // 2) as i:
                for par in range(2):
                    chunk_pe(e, i * 2 + par, par, i, False)
            pe_join(e)
            with e.Fori(0, GROUPS) as g:
                group_pe(e, g)

        @block.scalar
        def _(e):
            for t in (*evac, exp_ready, *pt_evac, rstd_ready, turned_copy, hidden, weights_ready, rows_done,
                      gate_std, gate_exp, diag_act):
                e.sem_inc(t, OPEN)
            e.preload_act_table_set("natural_log_exp_and_others")
            e.wait_ge(setup_done, 1)
            for t in range(FIRST_ALL):
                if t == 1:
                    e.wait_ge(vb_zero, 1)
                round_act(e, t, has(t))
            with e.Fori(FIRST_ALL, FIRST_TURN) as t:
                round_act(e, t, (True,) * 3)
            with e.Fori(0, LEVELS) as i:
                t = i * UNROLL + FIRST_TURN
                round_act(e, t, (True,) * 3, i * 2, across=True)
                round_act(e, t + 1, (True,) * 3, i * 2 + 1, back=True)
                round_act(e, t + 2, (True,) * 3)
            for t in range(STRIPS, ROUNDS):
                round_act(e, t, has(t))
            turn_tail_act(e)
            e.wait_ge(strip_saved, STRIPS + OPEN)
            e.wait_ge(experts_loaded, 16 * 5)
            with e.Fori(0, EPIECE // 2) as i:
                for par in range(2):
                    chunk_act(e, i * 2 + par, par, i, True)
            with e.Fori(EPIECE // 2, (EPIECE + TPIECE) // 2) as i:
                for par in range(2):
                    chunk_act(e, i * 2 + par, par, i, False)
            e.preload_act_table_set("natural_log_exp_and_others")
            act_join(e)
            for part in range(2):
                gates_act(e, 0, part)
            e.wait_ge(gates_ready, 1 + OPEN)
            for k in range(2):
                diagonals_act(e, 0, 0, k)
            with e.Fori(0, GROUPS // 2 - 1) as i:
                for par in range(2):
                    group_act(e, i * 2 + par, par, True)
            for g in range(GROUPS - 2, GROUPS):
                group_act(e, g, g % 2, g < GROUPS - 1)

        @block.gpsimd
        def _(e):
            for t in (xn_done, centered, probs_ready, idx_ready, idx_d_ready):
                e.sem_inc(t, OPEN)
            e.iota(loops_i[:, 0], [[-P, 32], [-EC, 8]], base=M - 1 + (KEY_BASE), channel_multiplier=-1
                   ).then_inc(self_loops, 1)
            e.wait_ge(vec_sums, 2)
            e.memset(vb[:, :, :, :, :], 0.0).then_inc(vb_zero, 1)
            for t in range(FIRST_ALL):
                round_pool(e, t, t, has(t))
            with e.Fori(0, (STRIPS - FIRST_ALL) // UNROLL) as i:
                for k in range(FIRST_ALL, FIRST_ALL + UNROLL):
                    round_pool(e, i * UNROLL + k, k % UNROLL, (True,) * 3)
            for t in range(STRIPS, ROUNDS):
                round_pool(e, t, t % UNROLL, has(t))
            e.wait_ge(strip_saved, STRIPS + OPEN)
            e.wait_ge(sorted_, 1)
            for n in range(2):
                e.indirect_dma_start(first[n][:, :], None, node_rows, bass.IndirectOffsetOnAxis(
                    ap=first_row_i[:, n:n + 1].bitcast(U32), axis=0)).then_inc(first_got, 16)
            with e.Fori(0, (EPIECE + TPIECE) // 2) as i:
                for par in range(2):
                    chunk_pool(e, i * 2 + par, par, i, (i * 2 + par) * U)
            pool_join(e)
            with e.Fori(0, GROUPS // 2) as i:
                for par in range(2):
                    group_pool(e, i * 2 + par, par, i)

        @block.sync
        def _(e):
            for t in (strip_saved, y_saved, rows_saved, fin_saved):
                e.sem_inc(t, OPEN)
            rest = REL - P
            loads = (
                (cst[:, :], const),
                (hot[:, 0, :], rel_hot[0:P, :]), (hot[0:rest, 1, :], rel_hot[P:REL, :]),
                (table_s[:, 0, :], bias_table[0:P, :]), (table_s[0:rest, 1, :], bias_table[P:REL, :]),
                (wq_s[:, :], wq_t), (wkv_s[:, :], wkv_t), (wproj_s[:, :], wproj_t),
                (vec[:, 0:1], bq.unsqueeze(1)), (vec[:, 1:2], bkv[0:C].unsqueeze(1)),
                (vec[:, 2:3], bkv[C:2 * C].unsqueeze(1)), (vec[:, 3:4], bproj.unsqueeze(1)),
                (wgat_s[:, :], w_gat),
                (att_s[:, 0:GC], att_src.rearrange("a b -> (a b)").partition_broadcast(P)),
                (att_s[:, GC:2 * GC], att_dst.rearrange("a b -> (a b)").partition_broadcast(P)),
                (gate_s[:, 0:GC], b_gat.partition_broadcast(P)),
                (gate_s[:, GC:2 * GC], ln_gamma.partition_broadcast(P)),
                (gate_s[:, 2 * GC:3 * GC], ln_beta.partition_broadcast(P)),
            )
            assert len(loads) == N_LOADS
            for dst, src in loads:
                e.dma_start(dst, src).then_inc(loaded, 16)
            for n in range(2):
                e.dma_start(edge_i[:, n, :], edges[n].rearrange("(p f) -> p f", p=P)).then_inc(edges_loaded, 16)
            xv = x.rearrange("b c h w -> c b (h w)")
            ov = out.rearrange("b c h w -> c b (h w)")
            nodes = node_rows.rearrange("(n p) r -> p n r", p=P)

            def row_of(s, j):
                r = s % 16
                return s // 16, (r * WS + SS if j == 0 else ((r + 1) % 16) * WS)

            def load_strip(s, par):
                for j in range(2):
                    img, row = row_of(s, j)
                    src = xv[:, bass.ds(img, 1), bass.ds(row * W, HTOK)] if not isinstance(s, int) else \
                        xv[:, img:img + 1, row * W:row * W + HTOK]
                    e.dma_start(xt[par][:, 4 * j:4 * j + 4, :].rearrange("c i w -> c (i w)"),
                                src.rearrange("c b t -> c (b t)")).then_inc(x_loaded[par], 16)

            def finish_strip(s, par, stores, more):
                t = s + 2
                wait_evac(e, t, 6)
                wait_evac(e, t, 7)
                if more:
                    load_strip(s + UNROLL, par)
                e.wait_ge(xn_done, t * 4 + 4 + OPEN)
                e.wait_ge(node_done, t * 2 + 2 + OPEN)
                for j in range(2):
                    img, row = row_of(s, j)
                    n = img * H + row
                    rws = slice(4 * j, 4 * j + 4)
                    at = bass.ds(n * W, HTOK)
                    e.dma_start(x1_dram[:, at], x1[par][:, rws, :].rearrange("c i w -> c (i w)")
                                ).then_inc(strip_stored[par], 16)
                    e.dma_start(xn_dram[:, at], x2[par][:, rws, :].rearrange("c i w -> c (i w)")
                                ).then_inc(strip_stored[par], 16)
                    e.dma_start(nodes[:, bass.ds(n, 4), :], node[par][:, rws, :]).then_inc(strip_stored[par], 16)
                e.wait_ge(strip_stored[par], stores * 96)
                e.sem_inc(strip_saved, 1)

            e.wait_ge(keys_made, 1)
            for s in range(UNROLL):
                load_strip(s, s)
            with e.Fori(0, STRIPS // UNROLL - 1) as i:
                for k in range(UNROLL):
                    finish_strip(i * UNROLL + k, k, i + 1, True)
            for s in range(STRIPS - STRIPS % UNROLL - UNROLL, STRIPS):
                finish_strip(s, s % UNROLL, s // UNROLL + 1, s + UNROLL < STRIPS)

            for dst, src in ((w1_s[:, :, :], w1.rearrange("e c f -> c e f")),
                             (w2_s[:, :, 0, :], w2[:, 0:P, :].rearrange("e f c -> f e c")),
                             (w2_s[:, :, 1, :], w2[:, P:FF, :].rearrange("e f c -> f e c")),
                             (b1_s[:, :, :].rearrange("p e k -> p (e k)"), b1),
                             (b2_s[:, :, :].rearrange("p e c -> p (e c)"),
                              b2.rearrange("e c -> (e c)").partition_broadcast(P))):
                e.dma_start(dst, src).then_inc(experts_loaded, 16)

            main = edge_rows[0:EDGES, :].rearrange("(p f) r -> p f r", p=P)
            tail = edge_rows[EDGES:MERGED, :].rearrange("(p f) r -> p f r", p=P)

            def load_tokens(c, par):
                e.dma_start(xm[par][:, :], xn_dram[:, bass.ds(c * 512, 512)]).then_inc(xm_loaded[par], 16)

            def chunk_sp(c, par, i, piece, col, experts, more):
                if more:
                    e.wait_ge(up_full, c * 8 + 8 + OPEN)
                    load_tokens(c + 2, par)
                if experts:
                    e.wait_ge(y_evac[0], c * 2 + 2 + OPEN)
                    e.wait_ge(y_evac[1], c * 2 + 2 + OPEN)
                    e.dma_start(y_dram[bass.ds(c * 4, 4)].rearrange("h p f -> p h f"), yt[par][:, :, :]
                                ).then_inc(y_stored, 16)
                e.wait_ge(rows_done, c + 1 + OPEN)
                e.dma_start(piece[:, bass.ds(col, U), :], rows[par][:, :, :]).then_inc(rows_stored, 16)
                if experts:
                    e.wait_ge(y_stored, (c + 1) * 16)
                    e.sem_inc(y_saved, 1)
                e.wait_ge(rows_stored, (c + 1) * 16)
                e.sem_inc(rows_saved, 1)

            load_tokens(0, 0)
            load_tokens(1, 1)
            with e.Fori(0, EPIECE // 2 - 1) as i:
                for par in range(2):
                    chunk_sp(i * 2 + par, par, i, main, (i * 2 + par) * U, True, True)
            for par in range(2):
                c = EPIECE - 2 + par
                chunk_sp(c, par, c // 2, main, c * U, True, False)
            with e.Fori(EPIECE // 2, (EPIECE + TPIECE) // 2) as i:
                for par in range(2):
                    chunk_sp(i * 2 + par, par, i, tail, (i * 2 + par - EPIECE) * U, False, False)

            def load_quad(t, b):
                e.dma_start(yo[b][:, :, :], y_dram[bass.ds(t * 4, 4)].rearrange("h p f -> p h f")
                            ).then_inc(yo_loaded[b], 16)
                e.dma_start(res[b][:, :], x1_dram[:, bass.ds(t * 512, 512)]).then_inc(res_loaded[b], 16)

            def store_quad(t, b):
                e.wait_ge(fin_ready, t + 1 + OPEN)
                e.dma_start(ov[:, bass.ds(t // 32, 1), bass.ds((t % 32) * 512, 512)].rearrange("c b t -> c (b t)"),
                            fin[b][:, :]).then_inc(out_stored[b], 16)

            e.wait_ge(runs_joined, 1)
            e.wait_ge(run_put, 32)
            for b in range(DEEP):
                load_quad(b, b)
            with e.Fori(0, GROUPS * QUADS // DEEP - 1) as q:
                for b in range(DEEP):
                    store_quad(q * DEEP + b, b)
                    load_quad(q * DEEP + b + DEEP, b)
                    e.wait_ge(out_stored[b], (q + 1) * 16)
                    e.sem_inc(fin_saved, 1)
            for b in range(DEEP):
                store_quad(GROUPS * QUADS - DEEP + b, b)
                e.wait_ge(out_stored[b], GROUPS * QUADS // DEEP * 16)


def kernel(**inputs):
    import concourse.bacc as bacc
    from concourse.bass_utils import run_bass_kernel_spmd

    nc = bacc.Bacc("TRN2", target_bir_lowering=False, num_devices=1)
    laid = {
        "x": inputs["x"],
        "wq_t": np.asarray(inputs["L0_conv_Wq"]).T,
        "bq": inputs["L0_conv_bq"],
        "wkv_t": np.asarray(inputs["L0_conv_Wkv"]).T,
        "bkv": inputs["L0_conv_bkv"],
        "wproj_t": np.asarray(inputs["L0_conv_Wproj"]).T,
        "bproj": inputs["L0_conv_bproj"],
        "bias_table": inputs["L0_conv_bias_table"],
        "w_gat": inputs["L0_ffn_W_gat"],
        "att_src": inputs["L0_ffn_att_src"],
        "att_dst": inputs["L0_ffn_att_dst"],
        "b_gat": inputs["L0_ffn_b_gat"],
        "ln_gamma": inputs["L0_ffn_ln_gamma"],
        "ln_beta": inputs["L0_ffn_ln_beta"],
        "w1": inputs["L0_ffn_W1"],
        "b1": np.asarray(inputs["L0_ffn_b1"]).reshape(NE * 2, P).T,
        "w2": inputs["L0_ffn_W2"],
        "b2": inputs["L0_ffn_b2"],
        "edges": inputs["L0_ffn_edge_index"],
        "const": constants(),
        "rel_hot": relative_one_hot(),
    }
    arrays, args = {}, []
    for name, value in laid.items():
        a = np.ascontiguousarray(value)
        arrays[f"in_{name}"] = a
        args.append(nc.dram_tensor(f"in_{name}", a.shape, mybir.dt.from_np(a.dtype), kind="ExternalInput").ap())
    args.append(nc.dram_tensor("out", (IMGS, C, H, W), F32, kind="ExternalOutput").ap())
    program(nc, *args)
    r = run_bass_kernel_spmd(nc, [arrays], core_ids=[0])
    return r.results[0]["out"]
```
